# Optimizing a Trainium2 kernel written in Bass

```python
import numpy as np
import jax
import jax.numpy as jnp

def _softmax(x, axis=-1):
    return jax.nn.softmax(x, axis=axis)

def _gelu(x):
    return jax.nn.gelu(x, approximate=True)

def _silu(x):
    return jax.nn.silu(x)

def _sigmoid(x):
    return jax.nn.sigmoid(x)

def _layernorm(x, axis=-1, eps=1e-05):
    m = jnp.mean(x, axis=axis, keepdims=True)
    v = jnp.var(x, axis=axis, keepdims=True)
    return (x - m) / jnp.sqrt(v + eps)

def _scatter_add(tgt, idx, src, axis=0):
    return tgt.at[idx].add(src)

def _segment_sum(src, seg, n):
    return jax.ops.segment_sum(src, seg, n)
kernel_name = 'mk_decoder_postln_d2_seqx_r4_d329ac'

def setup_inputs(seed: int=0):
    np.random.seed(seed)
    _w = jnp.asarray

    def _rec_inputs():
        import jax
        import jax.numpy as jnp
        _rk = jax.random.key(seed)
        x = 0.0003765 + 1 * jax.random.normal(jax.random.fold_in(_rk, 1), (8, 256, 512), jnp.float32)
        _lenS = 256 - jax.random.randint(jax.random.fold_in(_rk, 7), (8,), 0, max(1, 256 // 4) + 1, jnp.int32)
        _lenS2 = 256 - jax.random.randint(jax.random.fold_in(_rk, 8), (8,), 0, max(1, 256 // 4) + 1, jnp.int32)
        _ctx_2048P = jax.random.normal(jax.random.fold_in(_rk, 11), (8, 16, 512), jnp.float32)
        _ctx_2048c = jax.random.dirichlet(jax.random.fold_in(_rk, 511), 0.3 * jnp.ones((16,), jnp.float32), (8, 256))
        _ctx_2048t = jnp.einsum('bsk,bkd->bsd', _ctx_2048c, _ctx_2048P)
        _ctx_2048t = _ctx_2048t * jax.lax.rsqrt(jnp.mean(jnp.square(_ctx_2048t)) + 1e-12) * 0.953939
        ctx_2048 = -0.000292821 + 1.00034 * (_ctx_2048t + 0.3 * jax.random.normal(jax.random.fold_in(_rk, 611), (8, 256, 512), jnp.float32))
        return (x, ctx_2048)
    x, ctx_2048 = _rec_inputs()

    def _L0_attn_setup():
        import jax, jax.numpy as jnp
        import numpy as np
        H = 16
        KVH = 4
        D = 128
        HID = 512
        EPS = 1e-06
        GROUPS = H // KVH

        def elu_plus_one(x):
            return jax.nn.elu(x) + 1.0

        def _repeat_kv(x, b, s):
            x = x.reshape(b, s, KVH, 1, D)
            x = jnp.broadcast_to(x, (b, s, KVH, GROUPS, D))
            return x.reshape(b, s, H * D)

        def _split_heads(x, b, s, nh):
            return x.reshape(b, s, nh, D).transpose(0, 2, 1, 3)
        key = jax.random.key(seed)
        ks = jax.random.split(key, 8)
        s = 0.02
        return {'hidden_states': jax.random.normal(ks[0], (2, 1024, HID), jnp.float32), 'Wq': jax.random.normal(ks[1], (H * D, HID), jnp.float32) * s, 'bq': jnp.zeros((H * D,), jnp.float32), 'Wk': jax.random.normal(ks[2], (KVH * D, HID), jnp.float32) * s, 'bk': jnp.zeros((KVH * D,), jnp.float32), 'Wv': jax.random.normal(ks[3], (KVH * D, HID), jnp.float32) * s, 'bv': jnp.zeros((KVH * D,), jnp.float32), 'Wo': jax.random.normal(ks[4], (HID, H * D), jnp.float32) * s}
    _L0_attn_all = _L0_attn_setup()
    _L0_attn_in = {k: v for k, v in _L0_attn_all.items() if k in ('Wq', 'bq', 'Wk', 'bk', 'Wv', 'bv', 'Wo')}
    del _L0_attn_all

    def _L0_xattn_setup():
        import jax, jax.numpy as jnp
        import numpy as np
        key = jax.random.key(seed)
        k1, k2, k3, k4, k5 = jax.random.split(key, 5)
        B, D_MODEL, L = (2, 256, 512)
        HEAD_DIM = 8
        H = D_MODEL // HEAD_DIM
        return {'k': jax.random.normal(k1, (B, D_MODEL, L), dtype=jnp.float32), 'v': jax.random.normal(k2, (B, D_MODEL, L), dtype=jnp.float32), 'q': jax.random.normal(k3, (B, D_MODEL, L), dtype=jnp.float32), 'ssm_kernel': jax.random.normal(k4, (H, L), dtype=jnp.float32), 'D': jax.random.normal(k5, (H,), dtype=jnp.float32), 'head_dim': HEAD_DIM}
    _L0_xattn_all = _L0_xattn_setup()
    _L0_xattn_in = {k: v for k, v in _L0_xattn_all.items() if k in ('ssm_kernel', 'D')}
    del _L0_xattn_all

    def _L0_ffn_setup():
        import jax, jax.numpy as jnp
        import numpy as np
        HIDDEN = 512
        INTER = 1408
        B, S = (2, 512)

        def _ternary(key, shape):
            return jax.random.randint(key, shape, -1, 2).astype(jnp.float32)
        key = jax.random.key(seed)
        ks = jax.random.split(key, 7)
        x = jax.random.normal(ks[0], (B, S, HIDDEN), dtype=jnp.float32)
        gate_w = _ternary(ks[1], (INTER, HIDDEN))
        up_w = _ternary(ks[2], (INTER, HIDDEN))
        down_w = _ternary(ks[3], (HIDDEN, INTER))
        gate_s = jax.random.uniform(ks[4], (INTER,), minval=0.01, maxval=0.1, dtype=jnp.float32)
        up_s = jax.random.uniform(ks[5], (INTER,), minval=0.01, maxval=0.1, dtype=jnp.float32)
        down_s = jax.random.uniform(ks[6], (HIDDEN,), minval=0.01, maxval=0.1, dtype=jnp.float32)
        return {'x': x, 'gate_w': gate_w, 'up_w': up_w, 'down_w': down_w, 'gate_s': gate_s, 'up_s': up_s, 'down_s': down_s}
    _L0_ffn_all = _L0_ffn_setup()
    _L0_ffn_in = {k: v for k, v in _L0_ffn_all.items() if k in ('gate_w', 'up_w', 'down_w', 'gate_s', 'up_s', 'down_s')}
    del _L0_ffn_all

    def _L1_attn_setup():
        import jax, jax.numpy as jnp
        import numpy as np
        D_MODEL = 512
        N_HEADS = 16
        HEAD_DIM = D_MODEL // N_HEADS
        LN_EPS = 1e-06
        NEG_INF = float('-inf')

        def _layernorm_scale_only(x, scale):
            mean = jnp.mean(x, axis=-1, keepdims=True)
            var = jnp.var(x, axis=-1, keepdims=True)
            return (x - mean) * jax.lax.rsqrt(var + LN_EPS) * scale
        key = jax.random.key(seed)
        ks = jax.random.split(key, 4)
        B, S = (2, 512)
        x = jax.random.normal(ks[0], (B, S, D_MODEL), dtype=jnp.float32)
        Wqkv = jax.random.normal(ks[1], (D_MODEL, 3 * D_MODEL), dtype=jnp.float32) * 0.02
        q_ln_scale = jnp.ones((D_MODEL,), dtype=jnp.float32)
        k_ln_scale = jnp.ones((D_MODEL,), dtype=jnp.float32)
        out_W = jax.random.normal(ks[2], (D_MODEL, D_MODEL), dtype=jnp.float32) * 0.02
        return {'x': x, 'Wqkv': Wqkv, 'q_ln_scale': q_ln_scale, 'k_ln_scale': k_ln_scale, 'out_W': out_W}
    _L1_attn_all = _L1_attn_setup()
    _L1_attn_in = {k: v for k, v in _L1_attn_all.items() if k in ('Wqkv', 'q_ln_scale', 'k_ln_scale', 'out_W')}
    del _L1_attn_all

    def _L1_xattn_setup():
        import jax, jax.numpy as jnp
        import numpy as np
        N_HEAD = 8
        key = jax.random.key(seed)
        k1, k2, k3 = jax.random.split(key, 3)
        B, D, L = (4, 256, 512)
        q = jax.random.normal(k1, (B, D, L), dtype=jnp.float32)
        k = jax.random.normal(k2, (B, D, L), dtype=jnp.float32)
        v = jax.random.normal(k3, (B, D, L), dtype=jnp.float32)
        gamma = jnp.ones((), dtype=jnp.float32)
        return {'q': q, 'k': k, 'v': v, 'gamma': gamma}
    _L1_xattn_all = _L1_xattn_setup()
    _L1_xattn_in = {k: v for k, v in _L1_xattn_all.items() if k in ('gamma',)}
    del _L1_xattn_all

    def _L1_ffn_setup():
        import jax, jax.numpy as jnp
        import numpy as np
        D = 512
        E = 8
        R = 16
        K = 2
        INIT_BONUS = 3.0
        ANNEAL_STEPS = 1250
        CURRENT_STEP = 1
        key = jax.random.key(seed)
        ks = jax.random.split(key, 7)
        s_in = 1.0 / np.sqrt(D)
        s_r = 1.0 / np.sqrt(R)
        return {'x': jax.random.normal(ks[0], (2, 1024, D), dtype=jnp.float32), 'Wr': jax.random.normal(ks[1], (D, E), dtype=jnp.float32) * s_in, 'br': jax.random.normal(ks[2], (E,), dtype=jnp.float32) * 0.01, 'Wd': jax.random.normal(ks[3], (E, D, R), dtype=jnp.float32) * s_in, 'bd': jnp.zeros((E, R), dtype=jnp.float32), 'Wu': jax.random.normal(ks[4], (E, R, D), dtype=jnp.float32) * s_r, 'bu': jnp.zeros((E, D), dtype=jnp.float32)}
    _L1_ffn_all = _L1_ffn_setup()
    _L1_ffn_in = {k: v for k, v in _L1_ffn_all.items() if k in ('Wr', 'br', 'Wd', 'bd', 'Wu', 'bu')}
    del _L1_ffn_all
    return {'x': x, 'ctx_2048': ctx_2048, 'L0_attn_Wq': _L0_attn_in['Wq'], 'L0_attn_bq': _L0_attn_in['bq'], 'L0_attn_Wk': _L0_attn_in['Wk'], 'L0_attn_bk': _L0_attn_in['bk'], 'L0_attn_Wv': _L0_attn_in['Wv'], 'L0_attn_bv': _L0_attn_in['bv'], 'L0_attn_Wo': _L0_attn_in['Wo'], 'L0_xattn_ssm_kernel': _L0_xattn_in['ssm_kernel'], 'L0_xattn_D': _L0_xattn_in['D'], 'L0_ffn_gate_w': _L0_ffn_in['gate_w'], 'L0_ffn_up_w': _L0_ffn_in['up_w'], 'L0_ffn_down_w': _L0_ffn_in['down_w'], 'L0_ffn_gate_s': _L0_ffn_in['gate_s'], 'L0_ffn_up_s': _L0_ffn_in['up_s'], 'L0_ffn_down_s': _L0_ffn_in['down_s'], 'L1_attn_Wqkv': _L1_attn_in['Wqkv'], 'L1_attn_q_ln_scale': _L1_attn_in['q_ln_scale'], 'L1_attn_k_ln_scale': _L1_attn_in['k_ln_scale'], 'L1_attn_out_W': _L1_attn_in['out_W'], 'L1_xattn_gamma': _L1_xattn_in['gamma'], 'L1_ffn_Wr': _L1_ffn_in['Wr'], 'L1_ffn_br': _L1_ffn_in['br'], 'L1_ffn_Wd': _L1_ffn_in['Wd'], 'L1_ffn_bd': _L1_ffn_in['bd'], 'L1_ffn_Wu': _L1_ffn_in['Wu'], 'L1_ffn_bu': _L1_ffn_in['bu']}

def reference(x, ctx_2048, L0_attn_Wq, L0_attn_bq, L0_attn_Wk, L0_attn_bk, L0_attn_Wv, L0_attn_bv, L0_attn_Wo, L0_xattn_ssm_kernel, L0_xattn_D, L0_ffn_gate_w, L0_ffn_up_w, L0_ffn_down_w, L0_ffn_gate_s, L0_ffn_up_s, L0_ffn_down_s, L1_attn_Wqkv, L1_attn_q_ln_scale, L1_attn_k_ln_scale, L1_attn_out_W, L1_xattn_gamma, L1_ffn_Wr, L1_ffn_br, L1_ffn_Wd, L1_ffn_bd, L1_ffn_Wu, L1_ffn_bu):
    import jax
    import jax.numpy as jnp

    def _L0_attn_ref(hidden_states, Wq, bq, Wk, bk, Wv, bv, Wo):
        import jax, jax.numpy as jnp
        import numpy as np
        H = 16
        KVH = 4
        D = 128
        HID = 512
        EPS = 1e-06
        GROUPS = H // KVH

        def elu_plus_one(x):
            return jax.nn.elu(x) + 1.0

        def _repeat_kv(x, b, s):
            x = x.reshape(b, s, KVH, 1, D)
            x = jnp.broadcast_to(x, (b, s, KVH, GROUPS, D))
            return x.reshape(b, s, H * D)

        def _split_heads(x, b, s, nh):
            return x.reshape(b, s, nh, D).transpose(0, 2, 1, 3)
        b, s, _ = hidden_states.shape
        q = hidden_states @ Wq.T + bq
        k = hidden_states @ Wk.T + bk
        v = hidden_states @ Wv.T + bv
        k = _repeat_kv(k, b, s)
        v = _repeat_kv(v, b, s)
        q = _split_heads(q, b, s, H)
        k = _split_heads(k, b, s, H)
        v = _split_heads(v, b, s, H)
        sq = elu_plus_one(q)
        sk = elu_plus_one(k)
        kv = jnp.einsum('bhsd,bhse->bhde', sk, v)
        qkv = jnp.einsum('bhsd,bhde->bhse', sq, kv)
        k_sum = sk.sum(axis=2)
        norm = jnp.einsum('bhsd,bhd->bhs', sq, k_sum)
        attn = qkv / (norm[..., None] + EPS)
        attn = attn.transpose(0, 2, 1, 3).reshape(b, s, H * D)
        return attn @ Wo.T

    def _L0_xattn_ref(k, v, q, ssm_kernel, D, head_dim):
        import jax, jax.numpy as jnp
        import numpy as np
        B, HD, L = k.shape
        H = HD // head_dim
        fft_size = 2 * L
        k_ = k.reshape(B, H, head_dim, L)
        v_ = v.reshape(B, H, head_dim, L)
        q_ = q.reshape(B, H, head_dim, L)
        kv = jnp.einsum('bhil,bhjl->bijhl', k_, v_)
        kv_f = jnp.fft.rfft(kv, n=fft_size)
        kernel_f = jnp.fft.rfft(ssm_kernel, n=fft_size)
        y = jnp.fft.irfft(kv_f * kernel_f, n=fft_size)[..., :L]
        out = y + kv * D[None, None, None, :, None]
        out = jnp.einsum('bijhl,bhil->bjhl', out, q_)
        out = jnp.transpose(out, (0, 2, 1, 3)).reshape(B, H * head_dim, L)
        return out.astype(k.dtype)

    def _L0_ffn_ref(x, gate_w, up_w, down_w, gate_s, up_s, down_s):
        import jax, jax.numpy as jnp
        import numpy as np
        HIDDEN = 512
        INTER = 1408
        B, S = (2, 512)

        def _ternary(key, shape):
            return jax.random.randint(key, shape, -1, 2).astype(jnp.float32)
        b, s, h = x.shape
        xf = x.reshape(b * s, h)
        g = jnp.einsum('th,ih->ti', xf, gate_w) * gate_s
        u = jnp.einsum('th,ih->ti', xf, up_w) * up_s
        hdn = jax.nn.silu(g) * u
        out = jnp.einsum('ti,hi->th', hdn, down_w) * down_s
        return out.reshape(b, s, -1)

    def _L1_attn_ref(x, Wqkv, q_ln_scale, k_ln_scale, out_W):
        import jax, jax.numpy as jnp
        import numpy as np
        D_MODEL = 512
        N_HEADS = 16
        HEAD_DIM = D_MODEL // N_HEADS
        LN_EPS = 1e-06
        NEG_INF = float('-inf')

        def _layernorm_scale_only(x, scale):
            mean = jnp.mean(x, axis=-1, keepdims=True)
            var = jnp.var(x, axis=-1, keepdims=True)
            return (x - mean) * jax.lax.rsqrt(var + LN_EPS) * scale
        B, S, _ = x.shape
        qkv = jnp.einsum('bsd,de->bse', x, Wqkv)
        q, k, v = jnp.split(qkv, 3, axis=-1)
        q = _layernorm_scale_only(q, q_ln_scale)
        k = _layernorm_scale_only(k, k_ln_scale)
        q = q.reshape(B, S, N_HEADS, HEAD_DIM)
        k = k.reshape(B, S, N_HEADS, HEAD_DIM)
        v = v.reshape(B, S, N_HEADS, HEAD_DIM)
        scores = jnp.einsum('bshd,bthd->bhst', q / jnp.sqrt(jnp.float32(HEAD_DIM)), k)
        causal = jnp.triu(jnp.ones((S, S), dtype=bool), 1)
        scores = jnp.where(causal, NEG_INF, scores)
        attn = jax.nn.softmax(scores, axis=-1)
        ctx = jnp.einsum('bhst,bthd->bshd', attn, v)
        out = jnp.einsum('bsd,de->bse', ctx.reshape(B, S, D_MODEL), out_W)
        return out

    def _L1_xattn_ref(q, k, v, gamma):
        import jax, jax.numpy as jnp
        import numpy as np
        N_HEAD = 8
        B, Dq, Lq = q.shape
        Dv, Lk = (v.shape[-2], v.shape[-1])
        h = N_HEAD
        dq = Dq // h
        dv = Dv // h
        qh = q.reshape(B, h, dq, Lq)
        kh = k.reshape(B, h, dq, Lk)
        vh = v.reshape(B, h, dv, Lk)
        scale = 1.0 / jnp.sqrt(jnp.asarray(dq, dtype=q.dtype))
        qk = jnp.einsum('bhdq,bhdl->bhql', qh, kh) * scale
        sm = jax.nn.softmax(qk, axis=-1)
        ret = jnp.einsum('bhql,bhdl->bhdq', sm, vh)
        ret = ret.reshape(B, Dv, Lq)
        return gamma * ret

    def _L1_ffn_ref(x, Wr, br, Wd, bd, Wu, bu):
        import jax, jax.numpy as jnp
        import numpy as np
        D = 512
        E = 8
        R = 16
        K = 2
        INIT_BONUS = 3.0
        ANNEAL_STEPS = 1250
        CURRENT_STEP = 1
        logits = jnp.einsum('btd,de->bte', x, Wr) + br
        progress = min(CURRENT_STEP / ANNEAL_STEPS, 1.0)
        bonus = INIT_BONUS * (1.0 - progress)
        logits = logits + bonus
        gates = jax.nn.softmax(logits, axis=-1)
        topk_vals, topk_idx = jax.lax.top_k(gates, K)
        topk_vals = topk_vals / topk_vals.sum(axis=-1, keepdims=True)
        w = (jax.nn.one_hot(topk_idx, E, dtype=x.dtype) * topk_vals[..., None]).sum(axis=-2)
        h = jax.nn.relu(jnp.einsum('btd,edr->betr', x, Wd) + bd[None, :, None, :])
        eo = jnp.einsum('betr,erd->betd', h, Wu) + bu[None, :, None, :]
        out = jnp.einsum('bte,betd->btd', w, eo)
        return out
    x = _layernorm(x + _L0_attn_ref(x, L0_attn_Wq, L0_attn_bq, L0_attn_Wk, L0_attn_bk, L0_attn_Wv, L0_attn_bv, L0_attn_Wo), axis=-1)
    x = _layernorm(x + _L0_xattn_ref(ctx_2048, ctx_2048, x, L0_xattn_ssm_kernel, L0_xattn_D, 8), axis=-1)
    x = _layernorm(x + _L0_ffn_ref(x, L0_ffn_gate_w, L0_ffn_up_w, L0_ffn_down_w, L0_ffn_gate_s, L0_ffn_up_s, L0_ffn_down_s), axis=-1)
    x = _layernorm(x + _L1_attn_ref(x, L1_attn_Wqkv, L1_attn_q_ln_scale, L1_attn_k_ln_scale, L1_attn_out_W), axis=-1)
    x = _layernorm(x + _L1_xattn_ref(x, ctx_2048, ctx_2048, L1_xattn_gamma), axis=-1)
    x = _layernorm(x + _L1_ffn_ref(x, L1_ffn_Wr, L1_ffn_br, L1_ffn_Wd, L1_ffn_bd, L1_ffn_Wu, L1_ffn_bu), axis=-1)
    return x

_drawn_inputs = setup_inputs


def setup_inputs(seed=0):
    import zlib

    import numpy as np

    out = dict(_drawn_inputs(seed))
    spreads = {'L0_attn_bq': (0.0, 2.0),
     'L0_attn_bk': (0.0, 2.0),
     'L0_attn_bv': (0.0, 0.1),
     'L1_attn_q_ln_scale': (1.0, 0.2),
     'L1_attn_k_ln_scale': (1.0, 0.2),
     'L1_ffn_bd': (0.0, 0.1),
     'L1_ffn_bu': (0.0, 0.1)}
    factors = {'L0_attn_Wq': 89.958, 'L0_attn_Wk': 9.673}
    for name, (base, spread) in spreads.items():
        noise = np.random.default_rng([zlib.crc32(name.encode()), seed]).standard_normal(out[name].shape)
        drawn = base * np.exp(spread * noise) if base else spread * noise
        out[name] = jnp.asarray(drawn.astype(out[name].dtype))
    for name, factor in factors.items():
        out[name] = (out[name] * factor).astype(out[name].dtype)
    return out
```

```python
from contextlib import ExitStack

import concourse.bass as bass
from concourse import mybir

P = 128
B, S, D = 8, 256, 512
T = S // P
KT = D // P
EPS = 1e-5
RING = 3 * 2 * D

F32 = mybir.dt.float32
F32R = mybir.dt.float32r
ALU = mybir.AluOpType
ACT = mybir.ActivationFunctionType
AX = mybir.AxisListType


class Core:

    def __init__(self, nc, ctx):
        self.nc = nc
        self.sems = []
        self.x0 = ctx.enter_context(nc.sbuf_tensor("x0", [P, T, D], F32))
        self.ring = ctx.enter_context(nc.sbuf_tensor("ring", [P, RING], F32))
        self.ident = ctx.enter_context(nc.sbuf_tensor("ident", [P, P], F32))
        self.minus_half = ctx.enter_context(nc.sbuf_tensor("minus_half", [P, T], F32))
        self.eps = ctx.enter_context(nc.sbuf_tensor("eps", [P, T], F32))

    def sem(self, name):
        self.sems.append(self.nc.alloc_semaphore(name=name))
        return self.sems[-1]

    def clear(self):
        self.nc.clear_and_free_semaphores(self.sems)
        self.nc.all_engine_barrier()
        self.sems = []


def ints(x):
    return isinstance(x, int)


def rows(dram, b):
    return dram[bass.ds(b * S, S), :].rearrange("(t p) d -> p t d", p=P)


def wait_from(eng, sem, value):
    if not (ints(value) and value <= 0):
        eng.wait_ge(sem, value)


def over_batches(eng, body, tail=None):
    body(0, 0, True, False)
    with eng.Fori(0, (B - 2) // 2) as i:
        body(2 * i + 1, 1, False, False)
        body(2 * i + 2, 0, False, False)
    body(B - 1, 1, False, True)
    if tail:
        tail(B, 0)


def three_pass(pe, out, whi, wlo, xhi, xlo, start, stop):
    pe.matmul(out, whi, xhi, start=start, stop=False)
    pe.matmul(out, whi, xlo, start=False, stop=False)
    return pe.matmul(out, wlo, xhi, start=False, stop=stop)


class Split:
    def __init__(self, core, name, ahead, parts):
        self.pieces = [(dram, hi, lo) for dram, (hi, lo) in zip(ahead.weights, parts, strict=True)]
        self.buf, self.depth, self.loaded = ahead.buf, ahead.depth, ahead.loaded
        self.hi_done = core.sem(f"{name}_hi_done")
        self.lo_done = core.sem(f"{name}_lo_done")

    def load(self, sp, start=0, end=None):
        for n in range(max(start, self.depth), end or len(self.pieces)):
            sp.wait_ge(self.lo_done, n - self.depth + 1)
            sp.dma_start(self.buf(n), self.pieces[n][0]).then_inc(self.loaded[n % self.depth], 16)

    def round_hi(self, act, start, end):
        for n in range(start, end):
            act.wait_ge(self.loaded[n % self.depth], 16 * (n // self.depth + 1))
            act.activation(self.pieces[n][1], self.buf(n), ACT.Copy).then_inc(self.hi_done, 1)

    def take_lo(self, dve, start, end):
        for n in range(start, end):
            dve.wait_ge(self.hi_done, n + 1)
            dve.tensor_tensor(self.pieces[n][2], self.buf(n), self.pieces[n][1], ALU.subtract).then_inc(self.lo_done, 1)


class Ahead:

    def __init__(self, core, name, src, weights=(), size=RING):
        self.core, self.src, self.weights, self.size, self.depth = core, src, weights, size, RING // size
        self.x_loaded = core.nc.alloc_semaphore(name=f"{name}_x_loaded0")
        self.loaded = [core.nc.alloc_semaphore(name=f"{name}_w_loaded{i}") for i in range(self.depth if weights else 0)]

    def buf(self, n):
        _, blocks, width = self.weights[n].shape
        start = n % self.depth * self.size
        return self.core.ring[:, start:start + blocks * width].rearrange("p (a n) -> p a n", a=blocks)

    def load_x(self, sp):
        sp.dma_start(self.core.x0[:], rows(self.src, 0)).then_inc(self.x_loaded, 16)

    def load_weights(self, sp):
        for n in range(min(self.depth, len(self.weights))):
            sp.dma_start(self.buf(n), self.weights[n]).then_inc(self.loaded[n], 16)


def blocks_of(dram, first, count, cols):
    return dram[first * P:(first + count) * P, cols].rearrange("(a p) n -> p a n", p=P)


class Transposed:
    def __init__(self, core, ctx, name, src, ahead):
        nc = core.nc
        self.core, self.src = core, src
        sb = lambda n, s, dt: ctx.enter_context(nc.sbuf_tensor(f"{name}_{n}", s, dt))
        self.x = [core.x0, sb("x1", [P, T, D], F32)]
        self.hi = [sb(f"xt_hi{u}", [P, KT, S], F32R) for u in range(2)]
        self.lo = [sb(f"xt_lo{u}", [P, KT, S], F32R) for u in range(2)]
        self.bank = ctx.enter_context(nc.psum_tensor(f"{name}_xt_psum", [P, 2, S], F32))
        self.loaded = [ahead.x_loaded, core.sem(f"{name}_x_loaded1")]
        self.turned = core.sem(f"{name}_x_turned")
        self.hi_done = core.sem(f"{name}_xt_hi_done")
        self.lo_done = core.sem(f"{name}_xt_lo_done")

    def load(self, sp, b, u):
        sp.dma_start(self.x[u][:], rows(self.src, b)).then_inc(self.loaded[u], 16)

    def wait_loaded(self, eng, b, u):
        eng.wait_ge(self.loaded[u], 16 * (b // 2) + 16 if ints(b) else 8 * (b - u) + 16)

    def turn(self, pe, b, u, halves=(0, 1)):
        self.wait_loaded(pe, b, u)
        for r in halves:
            wait_from(pe, self.lo_done, 2 * b + r)
            for k in range(2):
                for t in range(T):
                    kt = 2 * r + k
                    last = pe.transpose(self.bank[:, k, t * P:(t + 1) * P],
                                        self.x[u][:, t, kt * P:(kt + 1) * P], self.core.ident[:])
            last.then_inc(self.turned, 1)

    def round_hi(self, act, b, u, halves=(0, 1)):
        for r in halves:
            act.wait_ge(self.turned, 2 * b + r + 1)
            act.activation(self.hi[u][:, 2 * r:2 * r + 2, :], self.bank[:], ACT.Copy).then_inc(self.hi_done, 1)

    def take_lo(self, dve, b, u, halves=(0, 1)):
        for r in halves:
            dve.wait_ge(self.hi_done, 2 * b + r + 1)
            dve.tensor_tensor(self.lo[u][:, 2 * r:2 * r + 2, :], self.bank[:],
                              self.hi[u][:, 2 * r:2 * r + 2, :], ALU.subtract).then_inc(self.lo_done, 1)

    def wait_ready(self, pe, b):
        pe.wait_ge(self.lo_done, 2 * b + 2)


class Norm:

    def __init__(self, core, ctx, name, dst):
        nc = core.nc
        self.core, self.dst = core, dst
        sb = lambda n, s: ctx.enter_context(nc.sbuf_tensor(f"{name}_{n}", s, F32))
        self.r = sb("r", [P, T, D])
        self.stats = sb("stats", [P, T, 6])
        self.mv = sb("mv", [P, T, 2])
        self.rstd = sb("rstd", [P, T])
        self.added = core.sem(f"{name}_added")
        self.stats_done = core.sem(f"{name}_stats_done")
        self.stats_seen = core.sem(f"{name}_stats_seen")
        self.mv_done = core.sem(f"{name}_mv_done")
        self.eps_added = core.sem(f"{name}_eps_added")
        self.rstd_done = core.sem(f"{name}_rstd_done")
        self.y_done = core.sem(f"{name}_y_done")
        self.stored = core.sem(f"{name}_stored")

    def statistics(self, dve, b, written=None, r=None):
        for t in range(T):
            dve.wait_ge(*(written[t] if written else (self.added, T * b + t + 1)))
            dve.bn_stats(self.stats[:, t, :], (r or self.r)[:, t, :]).then_inc(self.stats_done, 1)
        dve.wait_ge(self.stats_done, T * b + T)
        dve.sem_inc(self.stats_seen, 1)
        for t in range(T):
            dve.bn_aggr(self.mv[:, t, :], self.stats[:, t, :]).then_inc(self.mv_done, 1)

    def power(self, pool, b):
        pool.wait_ge(self.mv_done, T * b + T)
        wait_from(pool, self.y_done, T * b)
        pool.tensor_tensor(self.rstd[:], self.mv[:, :, 1], self.core.eps[:], ALU.add).then_inc(self.eps_added, 1)
        pool.wait_ge(self.eps_added, b + 1)
        pool.tensor_tensor(self.rstd[:], self.rstd[:], self.core.minus_half[:], ALU.pow).then_inc(self.rstd_done, 1)

    def apply(self, dve, b, r=None):
        r = r or self.r
        dve.wait_ge(self.rstd_done, b + 1)
        for t in range(T):
            dve.tensor_scalar(r[:, t, :], r[:, t, :], self.mv[:, t, 0:1], self.rstd[:, t:t + 1],
                              ALU.subtract, ALU.mult).then_inc(self.y_done, 1)

    def wait_stored(self, eng, b):
        wait_from(eng, self.stored, 16 * b)

    def store(self, sp, b, row=None, r=None):
        sp.wait_ge(self.y_done, T * b + T)
        sp.dma_start(rows(self.dst, b if row is None else row), (r or self.r)[:]).then_inc(self.stored, 16)


def constants(core, after):
    nc = core.nc
    zeroed, made = core.sem("ident_zeroed"), core.sem("constants_made")
    with nc.Block() as block:
        @block.sync
        def _(sp):
            after.load_x(sp)
            after.load_weights(sp)

        @block.gpsimd
        def _(pool):
            pool.memset(core.ident[:], 0.0).then_inc(zeroed, 1)
            pool.memset(core.minus_half[:], -0.5).then_inc(made, 1)
            pool.memset(core.eps[:], EPS).then_inc(made, 1)
            pool.wait_ge(zeroed, 1)
            pool.affine_select(out=core.ident[:], in_=core.ident[:], compare_op=ALU.not_equal, fill=1.0,
                               base=0, pattern=[[-1, P]], channel_multiplier=1).then_inc(made, 1)
            pool.wait_ge(made, 3)


H0, KVH, HD = 16, 4, 128
EPS0 = 1e-6


def kv_weights(wkT, wvT):
    return [blocks_of(src, k, 2, slice(0, KVH * HD)) for src in (wkT, wvT) for k in (0, 2)]


def qo_weights(wqT, woT):
    return [piece for p in range(H0 // 2) for piece in (
        blocks_of(wqT, 0, KT, slice(2 * p * HD, (2 * p + 2) * HD)), blocks_of(woT, 2 * p, 2, slice(0, D)))]


def l0_keys_values(core, ahead, after, kv, x, bk, bv):
    nc = core.nc
    with ExitStack() as ctx:
        sb = lambda n, s, dt=F32: ctx.enter_context(nc.sbuf_tensor(n, s, dt))
        pb = lambda n, s: ctx.enter_context(nc.psum_tensor(n, s, F32))
        W = KVH * HD
        wk = [sb(f"wk_{x}", [P, KT, W], F32R) for x in ("hi", "lo")]
        wv = [sb(f"wv_{x}", [P, KT, W], F32R) for x in ("hi", "lo")]
        split = Split(core, "wkv", ahead, [(w[0][:, k:k + 2, :], w[1][:, k:k + 2, :]) for w in (wk, wv) for k in (0, 2)])
        xt = Transposed(core, ctx, "a1", x, ahead)
        bk_row, bv_row = sb("bk_row", [P, W]), sb("bv_row", [P, W])
        kb = sb("kb", [P, T, W])
        sk = sb("sk", [P, T, W])
        v1 = sb("v1", [P, T, KVH, HD + 1])
        k_ps = [pb(f"k_ps{t}", [P, W]) for t in range(T)]
        v_ps = [pb(f"v_ps{t}", [P, W]) for t in range(T)]
        kv_ps = [pb(f"kv_ps{j}", [P, 2, 256]) for j in range(2)]
        bias_loaded, ones_set = core.sem("bkv_loaded"), core.sem("ones_set")
        k_mm, v_mm, kv_mm = core.sem("k_mm"), core.sem("v_mm"), core.sem("kv_mm")
        kb_done, mk_done, ek_done, sk_done = (core.sem(n) for n in ("kb_done", "mk_done", "ek_done", "sk_done"))
        v_done, kv_done = core.sem("v_done"), core.sem("kv_done")

        with nc.Block() as block:
            @block.sync
            def _(sp):
                split.load(sp)
                sp.dma_start(bk_row[:], bk.partition_broadcast(P)).then_inc(bias_loaded, 16)
                sp.dma_start(bv_row[:], bv.partition_broadcast(P)).then_inc(bias_loaded, 16)
                xt.load(sp, 1, 1)

                def next_loads(b, u):
                    sp.wait_ge(xt.turned, 2 * b - 2)
                    xt.load(sp, b, u)
                with sp.Fori(1, B // 2) as i:
                    next_loads(2 * i, 0)
                    next_loads(2 * i + 1, 1)
                sp.wait_ge(xt.turned, 2 * B - 2)
                after.load_x(sp)
                sp.wait_ge(split.lo_done, len(split.pieces))
                after.load_weights(sp)

            @block.scalar
            def _(act):
                xt.round_hi(act, 0, 0)
                split.round_hi(act, 0, len(split.pieces))

                def copy_kv(b):
                    act.wait_ge(kv_mm, b + 1)
                    for j in range(2):
                        out = kv[:, bass.ds(b, 1), 2 * j:2 * j + 2, :].rearrange("p a g n -> p (a g) n")
                        act.activation(out, kv_ps[j][:, :, 0:HD + 1], ACT.Copy).then_inc(kv_done, 1)

                def body(b, u, first, last):
                    for t in range(T):
                        act.wait_ge(mk_done, T * b + t + 1)
                        act.activation(sk[:, t, :], sk[:, t, :], ACT.Exp).then_inc(ek_done, 1)
                    if not last:
                        xt.round_hi(act, b + 1, 1 - u, [0])
                    if not first:
                        copy_kv(b - 1)
                    if not last:
                        xt.round_hi(act, b + 1, 1 - u, [1])
                over_batches(act, body, lambda b, u: copy_kv(b - 1))

            @block.vector
            def _(dve):
                dve.memset(v1[:, :, :, HD:HD + 1], 1.0).then_inc(ones_set, 1)
                xt.take_lo(dve, 0, 0)
                split.take_lo(dve, 0, len(split.pieces))
                dve.wait_ge(bias_loaded, 32)

                def body(b, u, first, last):
                    for t in range(T):
                        dve.wait_ge(k_mm, T * b + t + 1)
                        wait_from(dve, sk_done, T * b - T + t + 1)
                        dve.tensor_tensor(kb[:, t, :], k_ps[t][:], bk_row[:], ALU.add).then_inc(kb_done, 1)
                    wait_from(dve, kv_mm, b)
                    for t in range(T):
                        dve.wait_ge(kb_done, T * b + t + 1)
                        dve.tensor_scalar(sk[:, t, :], kb[:, t, :], 0.0, None, ALU.min).then_inc(mk_done, 1)
                    for t in range(T):
                        dve.wait_ge(ek_done, T * b + t + 1)
                        dve.scalar_tensor_tensor(sk[:, t, :], kb[:, t, :], 1.0, sk[:, t, :],
                                                 ALU.add, ALU.max).then_inc(sk_done, 1)
                    for t in range(T):
                        if not last:
                            xt.take_lo(dve, b + 1, 1 - u, [t])
                        dve.wait_ge(v_mm, T * b + t + 1)
                        dve.tensor_tensor(v1[:, t, :, 0:HD], v_ps[t][:].rearrange("p (g e) -> p g e", g=KVH),
                                          bv_row[:].rearrange("p (g e) -> p g e", g=KVH), ALU.add).then_inc(v_done, 1)
                over_batches(dve, body)

            @block.tensor
            def _(pe):
                xt.turn(pe, 0, 0)

                def project(w, out, done, freed, b, u, tiles=range(T)):
                    for t in tiles:
                        wait_from(pe, freed, T * b - T + t + 1)
                        for k in range(KT):
                            ts = slice(t * P, (t + 1) * P)
                            last = three_pass(pe, out[t][:], xt.hi[u][:, k, ts], xt.lo[u][:, k, ts],
                                              w[0][:, k, :], w[1][:, k, :], k == 0, k == KT - 1)
                        last.then_inc(done, 1)

                def products(b):
                    pe.wait_ge(sk_done, T * b + T)
                    pe.wait_ge(v_done, T * b + T)
                    if not (ints(b) and b == 0):
                        pe.wait_ge(kv_done, 2 * b)
                    else:
                        pe.wait_ge(ones_set, 1)
                    for g in range(KVH):
                        for t in range(T):
                            last = pe.matmul(kv_ps[g // 2][:, g % 2, 0:HD + 1], sk[:, t, g * HD:(g + 1) * HD],
                                             v1[:, t, g, :], start=(t == 0), stop=(t == T - 1))
                    last.then_inc(kv_mm, 1)

                def body(b, u, first, last):
                    xt.wait_ready(pe, b)
                    if first:
                        pe.wait_ge(split.lo_done, len(split.pieces) // 2)
                    project(wk, k_ps, k_mm, kb_done, b, u)
                    if not first:
                        products(b - 1)
                    if first:
                        pe.wait_ge(split.lo_done, len(split.pieces))
                    for t in range(T):
                        if not last:
                            xt.turn(pe, b + 1, 1 - u, [t])
                        project(wv, v_ps, v_mm, v_done, b, u, [t])
                over_batches(pe, body, lambda b, u: products(b - 1))


def l0_attention(core, ahead, after, kv, x, y, bq):
    nc = core.nc
    NP = H0 // 2
    with ExitStack() as ctx:
        sb = lambda n, s, dt=F32: ctx.enter_context(nc.sbuf_tensor(n, s, dt))
        pb = lambda n, s: ctx.enter_context(nc.psum_tensor(n, s, F32))
        wq = [sb(f"wq_{x}", [P, KT, H0 * HD], F32R) for x in ("hi", "lo")]
        wo = [sb(f"wo_{x}", [P, H0, D], F32R) for x in ("hi", "lo")]
        split = Split(core, "wqo", ahead, [part for p in range(NP) for part in (
            [w[:, :, 2 * p * HD:(2 * p + 2) * HD] for w in wq], [w[:, 2 * p:2 * p + 2, :] for w in wo])])
        xt = Transposed(core, ctx, "a2", x, ahead)
        norm = Norm(core, ctx, "n1", y)
        bq_col, bq1 = sb("bq_col", [P, H0]), sb("bq1", [P, H0])
        ex = [sb(f"ex{j}", [P, 2, S]) for j in range(2)]
        at = sb("at", [P, T, 2 * HD])
        rn = sb("rn", [P, T, 2])
        th, tl = sb("th", [P, 2, S], F32R), sb("tl", [P, 2, S], F32R)
        q_ps = [pb(f"q_ps{j}", [P, 2, S]) for j in range(2)]
        a_ps = [pb(f"a_ps{t}", [P, 2, 256]) for t in range(T)]
        t_ps = pb("t_ps", [P, 2, S])
        o_ps = [pb(f"o_ps{t}", [P, D]) for t in range(T)]
        bq_loaded, bq1_set = core.sem("bq_loaded"), core.sem("bq1_set")
        q_mm, eq_done, mq_done, sq_done = (core.sem(n) for n in ("q_mm", "eq_done", "mq_done", "sq_done"))
        a_mm, dn_done, rn_done, at_done = (core.sem(n) for n in ("a_mm", "dn_done", "rn_done", "at_done"))
        t_mm, th_done, tl_done, o_mm = (core.sem(n) for n in ("t_mm", "th_done", "tl_done", "o_mm"))

        def steps(b, first):
            for p in range(NP):
                yield p, ([(b, p - 1)] if p else [] if first else [(b - 1, NP - 1)]), \
                    ([(b, p - 2)] if p >= 2 else [] if first else [(b - 1, NP - 2 + p)])

        with nc.Block() as block:
            @block.sync
            def _(sp):
                sp.dma_start(bq_col[:], bq).then_inc(bq_loaded, 16)
                split.load(sp, 0, 4)
                xt.load(sp, 1, 1)
                split.load(sp, 4)

                def body(b, u, first, last):
                    norm.store(sp, b)
                    if not last and not (ints(b) and b >= B - 2):
                        xt.load(sp, b + 2, u)
                body(0, 0, True, False)
                with sp.Fori(0, (B - 4) // 2) as i:
                    body(2 * i + 1, 1, False, False)
                    body(2 * i + 2, 0, False, False)
                body(B - 3, 1, False, False)
                body(B - 2, 0, False, True)
                sp.wait_ge(norm.stored, 16)
                after.load_x(sp)
                after.load_weights(sp)
                body(B - 1, 1, False, True)
                sp.wait_ge(norm.stored, 16 * B)

            @block.gpsimd
            def _(pool):
                def body(b, u, first, last):
                    norm.power(pool, b)
                over_batches(pool, body)

            @block.scalar
            def _(act):
                xt.round_hi(act, 0, 0)
                split.round_hi(act, 0, 2)

                def scale(b, p):
                    n = NP * b + p
                    act.wait_ge(rn_done, n + 1)
                    wait_from(act, t_mm, n)
                    for t in range(T):
                        for h in range(2):
                            act.activation(at[:, t, h * HD:(h + 1) * HD], a_ps[t][:, h, 0:HD], ACT.Copy,
                                           scale=rn[:, t, h:h + 1]).then_inc(at_done, 1)

                def round_t(b, p):
                    n = NP * b + p
                    act.wait_ge(t_mm, n + 1)
                    wait_from(act, o_mm, n)
                    act.activation(th[:], t_ps[:], ACT.Copy).then_inc(th_done, 1)

                def body(b, u, first, last):
                    for p, attend, _ in steps(b, first):
                        n = NP * b + p
                        if first and p < NP - 1:
                            split.round_hi(act, 2 * p + 2, 2 * p + 4)
                        act.wait_ge(mq_done, 2 * n + 2)
                        act.activation(ex[p % 2][:], ex[p % 2][:], ACT.Exp).then_inc(eq_done, 1)
                        if p in (4, 6) and not last:
                            xt.round_hi(act, b + 1, 1 - u, [p // 2 - 2])
                        for c, r in attend:
                            scale(c, r)
                            round_t(c, r)

                def tail(b, u):
                    scale(b - 1, NP - 1)
                    round_t(b - 1, NP - 1)
                over_batches(act, body, tail)

            @block.vector
            def _(dve):
                dve.wait_ge(bq_loaded, 16)
                dve.tensor_scalar(bq1[:], bq_col[:], 1.0, None, ALU.add).then_inc(bq1_set, 1)
                xt.take_lo(dve, 0, 0)
                split.take_lo(dve, 0, 2)
                dve.wait_ge(bq1_set, 1)

                def reciprocals(b, p):
                    n = NP * b + p
                    dve.wait_ge(a_mm, n + 1)
                    wait_from(dve, at_done, 4 * n)
                    for t in range(T):
                        dve.tensor_scalar(rn[:, t, :], a_ps[t][:, :, HD], EPS0, None, ALU.add).then_inc(dn_done, 1)
                    dve.wait_ge(dn_done, T * n + T)
                    dve.reciprocal(rn[:], rn[:]).then_inc(rn_done, 1)

                def take_tl(b, p):
                    dve.wait_ge(th_done, NP * b + p + 1)
                    dve.tensor_tensor(tl[:], t_ps[:], th[:], ALU.subtract).then_inc(tl_done, 1)

                def finish(b, u):
                    dve.wait_ge(o_mm, NP * b + NP)
                    norm.wait_stored(dve, b)
                    for t in range(T):
                        dve.tensor_tensor(norm.r[:, t, :], o_ps[t][:], xt.x[u][:, t, :], ALU.add).then_inc(norm.added, 1)
                    norm.statistics(dve, b)

                def body(b, u, first, last):
                    for p, attend, _ in steps(b, first):
                        n = NP * b + p
                        if first and p < NP - 1:
                            split.take_lo(dve, 2 * p + 2, 2 * p + 4)
                        if p == 2 and not first:
                            finish(b - 1, 1 - u)
                        dve.wait_ge(q_mm, n + 1)
                        wait_from(dve, a_mm, n - 1)
                        for h in range(2):
                            head = 2 * p + h
                            dve.tensor_scalar(ex[p % 2][:, h, :], q_ps[p % 2][:, h, :], bq_col[:, head:head + 1],
                                              0.0, ALU.add, ALU.min).then_inc(mq_done, 1)
                        for c, r in attend:
                            reciprocals(c, r)
                        dve.wait_ge(eq_done, n + 1)
                        for h in range(2):
                            head = 2 * p + h
                            dve.scalar_tensor_tensor(ex[p % 2][:, h, :], q_ps[p % 2][:, h, :],
                                                     bq1[:, head:head + 1], ex[p % 2][:, h, :],
                                                     ALU.add, ALU.max).then_inc(sq_done, 1)
                        if p in (4, 6) and not last:
                            xt.take_lo(dve, b + 1, 1 - u, [p // 2 - 2])
                        for c, r in attend:
                            take_tl(c, r)
                        if p == 2 and not first:
                            norm.apply(dve, b - 1)

                def tail(b, u):
                    reciprocals(b - 1, NP - 1)
                    take_tl(b - 1, NP - 1)
                    finish(b - 1, 1 - u)
                    norm.apply(dve, b - 1)
                over_batches(dve, body, tail)

            @block.tensor
            def _(pe):
                xt.turn(pe, 0, 0)

                def project_q(b, u, p):
                    n = NP * b + p
                    wait_from(pe, sq_done, 2 * n - 2)
                    for h in range(2):
                        cols = slice((2 * p + h) * HD, (2 * p + h + 1) * HD)
                        for k in range(KT):
                            last = three_pass(pe, q_ps[p % 2][:, h, :], wq[0][:, k, cols], wq[1][:, k, cols],
                                              xt.hi[u][:, k, :], xt.lo[u][:, k, :], k == 0, k == KT - 1)
                    last.then_inc(q_mm, 1)

                def attend(b, p):
                    n = NP * b + p
                    pe.wait_ge(sq_done, 2 * n + 2)
                    wait_from(pe, at_done, 4 * n)
                    g = 2 * p // (H0 // KVH)
                    rhs = kv[:, bass.ds(b, 1), g, :].rearrange("p a n -> p (a n)")
                    for t in range(T):
                        for h in range(2):
                            last = pe.matmul(a_ps[t][:, h, 0:HD + 1], ex[p % 2][:, h, t * P:(t + 1) * P], rhs,
                                             start=True, stop=True)
                    last.then_inc(a_mm, 1)

                def turn(b, p):
                    n = NP * b + p
                    pe.wait_ge(at_done, 4 * n + 4)
                    wait_from(pe, tl_done, n)
                    for h in range(2):
                        for t in range(T):
                            last = pe.transpose(t_ps[:, h, t * P:(t + 1) * P], at[:, t, h * HD:(h + 1) * HD],
                                                core.ident[:])
                    last.then_inc(t_mm, 1)

                def project_out(b, p):
                    n = NP * b + p
                    pe.wait_ge(tl_done, n + 1)
                    if p == 0:
                        wait_from(pe, norm.added, T * b)
                    for t in range(T):
                        for h in range(2):
                            ts = slice(t * P, (t + 1) * P)
                            last = three_pass(pe, o_ps[t][:], th[:, h, ts], tl[:, h, ts],
                                              wo[0][:, 2 * p + h, :], wo[1][:, 2 * p + h, :],
                                              p == 0 and h == 0, p == NP - 1 and h == 1)
                    last.then_inc(o_mm, 1)

                def body(b, u, first, last):
                    xt.wait_ready(pe, b)
                    for p, now, before in steps(b, first):
                        if first:
                            pe.wait_ge(split.lo_done, 2 * p + 2)
                        project_q(b, u, p)
                        for c, r in now:
                            attend(c, r)
                        for c, r in before:
                            project_out(c, r)
                        for c, r in now:
                            turn(c, r)
                        if p in (3, 5) and not last:
                            xt.turn(pe, b + 1, 1 - u, [(p - 3) // 2])

                def tail(b, u):
                    attend(b - 1, NP - 1)
                    project_out(b - 1, NP - 2)
                    turn(b - 1, NP - 1)
                    project_out(b - 1, NP - 1)
                over_batches(pe, body, tail)


HC, HI = 32, 8
PAIRS = HI * (HI + 1) // 2
NCOL = PAIRS * B
LB = D // P
RUN = [(HI - d) * B for d in range(HI)]
OFF = [sum(RUN[:d]) for d in range(HI)]
HB = HI * B
PAD = P


def over(eng, n, body, tail=None):
    body(0, 0, True, False)
    with eng.Fori(0, (n - 2) // 2) as i:
        body(2 * i + 1, 1, False, False)
        body(2 * i + 2, 0, False, False)
    body(n - 1, 1, False, True)
    if tail:
        tail(n, 0)


def l0_convolution(core, ahead, after, x, ctx_rev, y, kernel, dskip, padded):
    nc = core.nc
    with ExitStack() as ctx:
        sb = lambda n, s, dt=F32: ctx.enter_context(nc.sbuf_tensor(n, s, dt))
        ct = sb("ct", [P, LB, S, B])
        qt = sb("qt", [P, LB, S, B])
        ot = sb("ot", [P, B, LB, S])
        l0_conv_turn(core, ahead, x, ctx_rev, ct, qt, kernel, dskip, padded)
        l0_conv_heads(core, ct, qt, ot, padded)
        l0_conv_norm(core, after, x, ot, y)


def l0_conv_turn(core, ahead, x, ctx_rev, ct, qt, kernel, dskip, padded):
    nc = core.nc
    with ExitStack() as ctx:
        sb = lambda n, s, dt=F32: ctx.enter_context(nc.sbuf_tensor(n, s, dt))
        kpad = sb("kpad", [HC, PAD + D])
        dcol = sb("dcol", [HC, 1])
        src = {"c": [ahead.buf(0), sb("c_tok1", [P, T, D])], "q": [core.x0, sb("q_tok1", [P, T, D])]}
        ps = {n: [[ctx.enter_context(nc.psum_tensor(f"{n}_turn_ps{u}{r}", [P, 2, S], F32)) for r in range(2)]
                  for u in range(2)] for n in "cq"}
        loaded = {"c": [ahead.loaded[0], core.sem("c_tok_loaded1")], "q": [ahead.x_loaded, core.sem("q_tok_loaded1")]}
        turned = {n: core.sem(f"{n}_tok_turned") for n in "cq"}
        copied = {n: core.sem(f"{n}_t_copied") for n in "cq"}
        kpad_zeroed, kern_loaded, d_added, kpad_stored = (core.sem(n) for n in (
            "kpad_zeroed", "kern_loaded", "d_added", "kpad_stored"))

        def copy(eng, n, dst, do):
            def body(b, u, first, last):
                for r in range(2):
                    eng.wait_ge(turned[n], 2 * b + r + 1)
                    out = dst[:, 2 * r:2 * r + 2, :, bass.ds(b, 1)].rearrange("p k s b -> p k (s b)")
                    do(out, ps[n][u][r][:]).then_inc(copied[n], 1)
            over_batches(eng, body)

        with nc.Block() as block:
            @block.sync
            def _(sp):
                sp.wait_ge(kpad_zeroed, 1)
                sp.dma_start(kpad[:, PAD:PAD + D], kernel).then_inc(kern_loaded, 16)
                sp.dma_start(dcol[:], dskip).then_inc(kern_loaded, 16)

                def body(b, u, first, last):
                    for n, dram in (("c", ctx_rev), ("q", x)):
                        if first:
                            continue
                        wait_from(sp, turned[n], 2 * b - 2)
                        sp.dma_start(src[n][u][:], rows(dram, b)).then_inc(loaded[n][u], 16)
                over_batches(sp, body)
                sp.wait_ge(d_added, 1)
                sp.dma_start(padded, kpad[:]).then_inc(kpad_stored, 16)
                sp.wait_ge(kpad_stored, 16)

            @block.gpsimd
            def _(pool):
                pool.memset(kpad[:], 0.0).then_inc(kpad_zeroed, 1)

            @block.scalar
            def _(act):
                copy(act, "c", ct, lambda out, in_: act.activation(out, in_, ACT.Copy))

            @block.vector
            def _(dve):
                dve.wait_ge(kern_loaded, 32)
                dve.tensor_tensor(kpad[:, PAD:PAD + 1], kpad[:, PAD:PAD + 1], dcol[:], ALU.add).then_inc(d_added, 1)
                copy(dve, "q", qt, lambda out, in_: dve.tensor_copy(out, in_))

            @block.tensor
            def _(pe):
                def body(b, u, first, last):
                    for n in "cq":
                        pe.wait_ge(loaded[n][u], 16 * (b // 2) + 16 if ints(b) else 8 * (b - u) + 16)
                        wait_from(pe, copied[n], 2 * b - 2)
                        for r in range(2):
                            for k in range(2):
                                for t in range(T):
                                    kt = 2 * r + k
                                    last_mm = pe.transpose(ps[n][u][r][:, k, t * P:(t + 1) * P],
                                                           src[n][u][:, t, kt * P:(kt + 1) * P], core.ident[:])
                            last_mm.then_inc(turned[n], 1)
                over_batches(pe, body)


def l0_conv_heads(core, ct, qt, ot, padded):
    nc = core.nc
    with ExitStack() as ctx:
        sb = lambda n, s, dt=F32: ctx.enter_context(nc.sbuf_tensor(n, s, dt))
        toep = [sb(f"toep{u}", [P, D]) for u in range(2)]
        cc = [sb(f"cc{u}", [P, LB, NCOL]) for u in range(2)]
        ys = [sb(f"ys{u}", [P, LB, NCOL]) for u in range(2)]
        pr = [sb(f"pr{u}", [P, LB, HI, HB]) for u in range(2)]
        yp = [ctx.enter_context(nc.psum_tensor(f"yp{u}", [P, LB, 512], F32)) for u in range(2)]
        toep_loaded = [core.sem(f"toep_loaded{u}") for u in range(2)]
        cc_done, sq_done = core.sem("cc_done"), core.sem("conv_sq_done")
        conv_mm, ys_done = core.sem("conv_mm"), core.sem("ys_done")
        pr_done, fold_done, ot_done = core.sem("pr_done"), core.sem("fold_done"), core.sem("ot_done")

        with nc.Block() as block:
            @block.sync
            def _(sp):
                def body(h, u, first, last):
                    wait_from(sp, conv_mm, h - 1)
                    row = padded[bass.ds(h, 1), 1:1 + D]
                    windows = bass.AP(tensor=row.tensor, offset=row.offset, ap=[[1, P], [1, D]])
                    sp.dma_start(toep[u][:], windows).then_inc(toep_loaded[u], 16)
                over(sp, HC, body)

            @block.gpsimd
            def _(pool):
                def products(h, u):
                    wait_from(pool, conv_mm, h - 1)
                    for d in range(1, HI):
                        a, b = (ct[:, :, bass.ds(h * HI + e, HI - d), :].rearrange("p k i b -> p k (i b)") for e in (0, d))
                        last = pool.tensor_tensor(cc[u][:, :, OFF[d]:OFF[d] + RUN[d]], a, b, ALU.mult)
                    last.then_inc(cc_done, 1)

                def fold(h, u):
                    pool.wait_ge(pr_done, h + 1)
                    half = HI // 2
                    pool.tensor_tensor(pr[u][:, :, 0:half, :], pr[u][:, :, 0:half, :], pr[u][:, :, half:HI, :],
                                       ALU.add).then_inc(fold_done, 1)

                def body(h, u, first, last):
                    if not last:
                        products(h + 1, 1 - u)
                    if not first:
                        fold(h - 1, 1 - u)
                products(0, 0)
                over(pool, HC, body, lambda h, u: fold(h - 1, 1 - u))

            @block.scalar
            def _(act):
                def squares(h, u):
                    wait_from(act, conv_mm, h - 1)
                    c = ct[:, :, bass.ds(h * HI, HI), :].rearrange("p k i b -> p k (i b)")
                    act.activation(cc[u][:, :, OFF[0]:OFF[0] + RUN[0]], c, ACT.Square).then_inc(sq_done, 1)

                squares(0, 0)

                def body(h, u, first, last):
                    if not last:
                        squares(h + 1, 1 - u)
                    wait_from(act, pr_done, h - 1)
                    act.wait_ge(conv_mm, h + 1)
                    for lb in range(LB):
                        act.activation(ys[u][:, lb, :], yp[u][:, lb, 0:NCOL], ACT.Copy).then_inc(ys_done, 1)
                over(act, HC, body)

            @block.vector
            def _(dve):
                def terms(h, u):
                    dve.wait_ge(ys_done, LB * h + LB)
                    wait_from(dve, ot_done, h - 1)
                    for d in range(HI):
                        yd = ys[u][:, :, OFF[d]:OFF[d] + RUN[d]]
                        for e, r in ((0, d), (d, HI - d)):
                            if r == HI:
                                continue
                            q = qt[:, :, bass.ds(h * HI + e, HI - d), :].rearrange("p k i b -> p k (i b)")
                            lo = (d - e) * B
                            last = dve.tensor_tensor(pr[u][:, :, r, lo:lo + RUN[d]], yd, q, ALU.mult)
                    last.then_inc(pr_done, 1)

                def sums(h, u):
                    dve.wait_ge(fold_done, h + 1)
                    for lb in range(LB):
                        out = ot[:, :, lb, bass.ds(h * HI, HI)]
                        in_ = pr[u][:, lb, 0:HI // 2, :].rearrange("p r (j b) -> p b j r", b=B)
                        last = dve.tensor_reduce(out, in_, AX.X, ALU.add)
                    last.then_inc(ot_done, 1)

                def body(h, u, first, last):
                    terms(h, u)
                    if not first:
                        sums(h - 1, 1 - u)
                over(dve, HC, body, lambda h, u: sums(h - 1, 1 - u))

            @block.tensor
            def _(pe):
                def body(h, u, first, last):
                    pe.wait_ge(cc_done, h + 1)
                    pe.wait_ge(sq_done, h + 1)
                    pe.wait_ge(toep_loaded[u], 16 * (h // 2) + 16 if ints(h) else 8 * (h - u) + 16)
                    wait_from(pe, ys_done, LB * h - LB)
                    for lo in range(LB):
                        for li in range(lo + 1):
                            last_mm = pe.matmul(yp[u][:, lo, 0:NCOL], toep[u][:, (lo - li) * P:(lo - li + 1) * P],
                                                cc[u][:, li, :], start=(li == 0), stop=(li == lo))
                    last_mm.then_inc(conv_mm, 1)
                over(pe, HC, body)


def l0_conv_norm(core, after, x, ot, y):
    nc = core.nc
    with ExitStack() as ctx:
        xr = [ctx.enter_context(nc.sbuf_tensor(f"xr{b}", [P, T, D], F32)) for b in range(B)]
        ps = [[ctx.enter_context(nc.psum_tensor(f"ot_ps{u}{t}", [P, D], F32)) for t in range(T)] for u in range(2)]
        norms = [Norm(core, ctx, f"n2{u}", y) for u in range(2)]
        loaded = [core.sem(f"xr_loaded{b}") for b in range(B)]
        turned = core.sem("ot_turned")
        with nc.Block() as block:
            @block.sync
            def _(sp):
                for b in range(B):
                    sp.dma_start(xr[b][:], rows(x, b)).then_inc(loaded[b], 16)
                after.load_weights(sp)
                for b in range(B):
                    norms[b % 2].store(sp, b // 2, b, xr[b])
                    if b == 1:
                        sp.wait_ge(norms[0].stored, 16)
                        after.load_x(sp)
                for norm in norms:
                    sp.wait_ge(norm.stored, 16 * (B // 2))

            @block.gpsimd
            def _(pool):
                for b in range(B):
                    norms[b % 2].power(pool, b // 2)

            @block.tensor
            def _(pe):
                for b in range(B):
                    if b >= 2:
                        pe.wait_ge(norms[b % 2].added, T * (b // 2))
                    for t in range(T):
                        for k in range(LB):
                            last = pe.transpose(ps[b % 2][t][:, k * P:(k + 1) * P], ot[:, b, k, t * P:(t + 1) * P],
                                                core.ident[:])
                    last.then_inc(turned, 1)

            @block.vector
            def _(dve):
                for b in range(B):
                    norm = norms[b % 2]
                    dve.wait_ge(turned, b + 1)
                    dve.wait_ge(loaded[b], 16)
                    for t in range(T):
                        dve.tensor_tensor(xr[b][:, t, :], ps[b % 2][t][:], xr[b][:, t, :], ALU.add)\
                           .then_inc(norm.added, 1)
                    norm.statistics(dve, b // 2, r=xr[b])
                    if b >= 1:
                        norms[1 - b % 2].apply(dve, (b - 1) // 2, xr[b - 1])
                norms[(B - 1) % 2].apply(dve, (B - 1) // 2, xr[B - 1])


INTER = 1408
NJ = INTER // P


def ffn_weights(gateT, upT, downT):
    return [piece for j in range(NJ) for piece in (
        blocks_of(gateT, 0, KT, slice(j * P, (j + 1) * P)), blocks_of(upT, 0, KT, slice(j * P, (j + 1) * P)),
        blocks_of(downT, j, 1, slice(0, D)))]


def l0_feed_forward(core, ahead, after, x, y, gs, us, ds):
    nc = core.nc
    with ExitStack() as ctx:
        sb = lambda n, s, dt=F32: ctx.enter_context(nc.sbuf_tensor(n, s, dt))
        pb = lambda n, s: ctx.enter_context(nc.psum_tensor(n, s, F32))
        wg = [sb(f"wg_{x}", [P, KT, INTER], F32R) for x in ("hi", "lo")]
        wu = [sb(f"wu_{x}", [P, KT, INTER], F32R) for x in ("hi", "lo")]
        wd = [sb(f"wd_{x}", [P, NJ, D], F32R) for x in ("hi", "lo")]
        split = Split(core, "wgud", ahead, [part for j in range(NJ) for part in (
            [w[:, :, j * P:(j + 1) * P] for w in wg], [w[:, :, j * P:(j + 1) * P] for w in wu],
            [w[:, j:j + 1, :] for w in wd])])
        xt = Transposed(core, ctx, "c", x, ahead)
        norm = Norm(core, ctx, "n3", y)
        gs_col, us_col, ds_row = sb("gs_col", [P, NJ]), sb("us_col", [P, NJ]), sb("ds_row", [P, D])
        sg = [sb(f"sg{j}", [P, S]) for j in range(2)]
        hm = [sb(f"hm{j}", [P, S]) for j in range(2)]
        hh = [sb(f"hh{j}", [P, S], F32R) for j in range(2)]
        hl = [sb(f"hl{j}", [P, S], F32R) for j in range(2)]
        gu_ps = [pb(f"gu_ps{j}", [P, 2, S]) for j in range(2)]
        d_ps = [pb(f"d_ps{t}", [P, D]) for t in range(T)]
        scales_loaded = core.sem("scales_loaded")
        gu_mm, sg_done, hm_done, hh_done, hl_done, d_mm, d_scaled = (core.sem(n) for n in (
            "gu_mm", "sg_done", "hm_done", "hh_done", "hl_done", "d_mm", "d_scaled"))

        def before(b, j, first):
            return [(b, j - 1)] if j else [] if first else [(b - 1, NJ - 1)]

        with nc.Block() as block:
            @block.sync
            def _(sp):
                sp.dma_start(gs_col[:], gs).then_inc(scales_loaded, 16)
                sp.dma_start(us_col[:], us).then_inc(scales_loaded, 16)
                sp.dma_start(ds_row[:], ds.partition_broadcast(P)).then_inc(scales_loaded, 16)
                split.load(sp, 0, 12)
                xt.load(sp, 1, 1)
                split.load(sp, 12)

                def body(b, u, first, last):
                    norm.store(sp, b)
                    if not last:
                        xt.load(sp, b + 2, u)
                body(0, 0, True, False)
                with sp.Fori(0, (B - 4) // 2) as i:
                    body(2 * i + 1, 1, False, False)
                    body(2 * i + 2, 0, False, False)
                body(B - 3, 1, False, False)
                body(B - 2, 0, False, True)
                sp.wait_ge(norm.stored, 16)
                after.load_x(sp)
                after.load_weights(sp)
                body(B - 1, 1, False, True)
                sp.wait_ge(norm.stored, 16 * B)

            @block.gpsimd
            def _(pool):
                over_batches(pool, lambda b, u, first, last: norm.power(pool, b))

            @block.scalar
            def _(act):
                xt.round_hi(act, 0, 0)
                split.round_hi(act, 0, 3)
                act.wait_ge(scales_loaded, 48)

                def body(b, u, first, last):
                    for j in range(NJ):
                        n, v = NJ * b + j, (u + j) % 2
                        if first and j < NJ - 1:
                            split.round_hi(act, 3 * j + 3, 3 * j + 6)
                        act.wait_ge(gu_mm, n + 1)
                        wait_from(act, hm_done, n - 1)
                        act.activation(sg[v][:], gu_ps[v][:, 0, :], ACT.Silu, scale=gs_col[:, j:j + 1])\
                           .then_inc(sg_done, 1)
                        act.wait_ge(hm_done, n + 1)
                        wait_from(act, d_mm, n - 1)
                        act.activation(hh[v][:], hm[v][:], ACT.Copy).then_inc(hh_done, 1)
                        if j in (7, 9) and not last:
                            xt.round_hi(act, b + 1, 1 - u, [(j - 7) // 2])
                over_batches(act, body)

            @block.vector
            def _(dve):
                xt.take_lo(dve, 0, 0)
                split.take_lo(dve, 0, 3)
                dve.wait_ge(scales_loaded, 48)

                def finish(b, u):
                    dve.wait_ge(d_mm, NJ * b + NJ)
                    norm.wait_stored(dve, b)
                    for t in range(T):
                        dve.tensor_tensor(norm.r[:, t, :], d_ps[t][:], ds_row[:], ALU.mult).then_inc(d_scaled, 1)
                    for t in range(T):
                        dve.wait_ge(d_scaled, T * b + t + 1)
                        dve.tensor_tensor(norm.r[:, t, :], norm.r[:, t, :], xt.x[u][:, t, :], ALU.add)\
                           .then_inc(norm.added, 1)
                    norm.statistics(dve, b)

                def body(b, u, first, last):
                    for j in range(NJ):
                        n, v = NJ * b + j, (u + j) % 2
                        if first and j < NJ - 1:
                            split.take_lo(dve, 3 * j + 3, 3 * j + 6)
                        if j == 1 and not first:
                            finish(b - 1, 1 - u)
                        dve.wait_ge(sg_done, n + 1)
                        wait_from(dve, hl_done, n - 1)
                        dve.scalar_tensor_tensor(hm[v][:], gu_ps[v][:, 1, :], us_col[:, j:j + 1], sg[v][:],
                                                 ALU.mult, ALU.mult).then_inc(hm_done, 1)
                        dve.wait_ge(hh_done, n + 1)
                        dve.tensor_tensor(hl[v][:], hm[v][:], hh[v][:], ALU.subtract).then_inc(hl_done, 1)
                        if j == 2 and not first:
                            norm.apply(dve, b - 1)
                        if j in (7, 9) and not last:
                            xt.take_lo(dve, b + 1, 1 - u, [(j - 7) // 2])

                def tail(b, u):
                    finish(b - 1, 1 - u)
                    norm.apply(dve, b - 1)
                over_batches(dve, body, tail)

            @block.tensor
            def _(pe):
                xt.turn(pe, 0, 0)

                def gate_up(b, u, j):
                    n, v = NJ * b + j, (u + j) % 2
                    wait_from(pe, hm_done, n - 1)
                    cols = slice(j * P, (j + 1) * P)
                    for i, w in enumerate((wg, wu)):
                        for k in range(KT):
                            last = three_pass(pe, gu_ps[v][:, i, :], w[0][:, k, cols], w[1][:, k, cols],
                                              xt.hi[u][:, k, :], xt.lo[u][:, k, :], k == 0, k == KT - 1)
                    last.then_inc(gu_mm, 1)

                def down(b, u, j):
                    n, v = NJ * b + j, (u + j) % 2
                    pe.wait_ge(hl_done, n + 1)
                    if j == 0:
                        wait_from(pe, d_scaled, T * b)
                    for t in range(T):
                        ts = slice(t * P, (t + 1) * P)
                        last = three_pass(pe, d_ps[t][:], hh[v][:, ts], hl[v][:, ts], wd[0][:, j, :], wd[1][:, j, :],
                                          j == 0, j == NJ - 1)
                    last.then_inc(d_mm, 1)

                def body(b, u, first, last):
                    xt.wait_ready(pe, b)
                    for j in range(NJ):
                        if first:
                            pe.wait_ge(split.lo_done, 3 * j + 3)
                        gate_up(b, u, j)
                        for c, r in before(b, j, first):
                            down(c, u if r == j - 1 else 1 - u, r)
                        if j in (6, 8) and not last:
                            xt.turn(pe, b + 1, 1 - u, [(j - 6) // 2])
                over_batches(pe, body, lambda b, u: down(b - 1, 1 - u, NJ - 1))


H1, HD1 = 16, 32
NG, GH = 4, 4
EPS1 = 1e-6
NEG = -1e30


def qkvo_weights(wqkv, wout):
    return [blocks_of(wqkv, k, 2, slice(i * D, (i + 1) * D)) for i in range(3) for k in (0, 2)] + \
        [blocks_of(wout, k, 2, slice(0, D)) for k in (0, 2)]


def l1_attention(core, ahead, after, x, y, q_scale, k_scale):
    nc = core.nc
    with ExitStack() as ctx:
        sb = lambda n, s, dt=F32: ctx.enter_context(nc.sbuf_tensor(n, s, dt))
        pb = lambda n, s: ctx.enter_context(nc.psum_tensor(n, s, F32))
        w = [sb(f"wqkv_{x}", [P, KT, 3, D], F32R) for x in ("hi", "lo")]
        wo = [sb(f"wout_{x}", [P, KT, D], F32R) for x in ("hi", "lo")]
        split = Split(core, "wqkvo", ahead, [[part[:, k:k + 2, i, :] for part in w] for i in range(3) for k in (0, 2)]
                      + [[part[:, k:k + 2, :] for part in wo] for k in (0, 2)])
        xt = Transposed(core, ctx, "d", x, ahead)
        norm = Norm(core, ctx, "n4", y)
        qs_row, ks_row = sb("qs_row", [P, D]), sb("ks_row", [P, D])
        mask = sb("mask", [P, P])
        eps1, half2 = sb("eps1", [P, 2]), sb("half2", [P, 2])
        pos, neg = sb("pos_scale", [P, 1]), sb("neg_scale", [P, 1])
        qn = [sb(f"qn{t}", [P, D]) for t in range(T)]
        kn = [sb(f"kn{t}", [P, D]) for t in range(T)]
        st = sb("qk_stats", [P, T, 2, 6])
        mv = sb("qk_mv", [P, T, 2, 2])
        rstd = sb("qk_rstd", [P, T, 2])
        rq = [sb(f"rq{u}", [P, T]) for u in range(2)]
        nrq = [sb(f"nrq{u}", [P, T]) for u in range(2)]
        vt = [sb(f"vt{u}", [P, T, D]) for u in range(2)]
        qT = [sb(f"qT{u}", [P, NG, T, P]) for u in range(2)]
        kT = [sb(f"kT{u}", [P, NG, T, GH, P]) for u in range(2)]
        p0 = [sb(f"p0_{i}", [P, GH, P]) for i in range(2)]
        p1 = [sb(f"p1_{i}", [P, GH, S]) for i in range(2)]
        mx = [sb(f"mx{i}", [P, T, GH]) for i in range(2)]
        nb = [sb(f"nb{i}", [P, T, GH]) for i in range(2)]
        sums = [sb(f"sums{i}", [P, T, GH]) for i in range(2)]
        rs = [sb(f"rs{i}", [P, T, GH]) for i in range(2)]
        pT = [sb(f"pT{i}", [P, GH, S + P]) for i in range(2)]
        oh = [sb(f"oh{u}", [P, NG, S], F32R) for u in range(2)]
        ol = [sb(f"ol{u}", [P, NG, S], F32R) for u in range(2)]
        p_ps = [pb(f"p_ps{i}", [P, D]) for i in range(2)]
        s_ps = [pb(f"s_ps{i}", [P, GH, P]) for i in range(2)]
        t_ps = [pb(f"tr_ps{i}", [P, NG, P]) for i in range(2)]
        v_ps = pb("v_out_ps", [P, S])

        s = lambda n: core.sem("d_" + n)
        rows_loaded, set_up, mask_zeroed, xr_loaded = s("rows_loaded"), s("set_up"), s("mask_zeroed"), s("xr_loaded")
        p_mm, o_mm, p_free = s("p_mm"), s("o_mm"), [s("p_free0"), s("p_free1")]
        st_done, st_seen, mv_done, ve_done, rstd_done = (s(n) for n in (
            "st_done", "st_seen", "mv_done", "ve_done", "rstd_done"))
        rq_done, kn_done, qk_turned, t_free = s("rq_done"), s("kn_done"), s("qk_turned"), [s("t_free0"), s("t_free1")]
        s_mm, s_free = s("s_mm"), [s("s_free0"), s("s_free1")]
        mx_done, nb_done, e_done, rs_done, pn_done = (s(n) for n in (
            "mx_done", "nb_done", "e_done", "rs_done", "pn_done"))
        pt_mm, pv_mm, oh_done, ol_done = (s(n) for n in ("pt_mm", "pv_mm", "oh_done", "ol_done"))

        def d_over(eng, body, tail):
            body(0, 0, True, False)
            body(1, 1, False, False)
            with eng.Fori(0, (B - 4) // 2) as i:
                body(2 * i + 2, 0, False, False)
                body(2 * i + 3, 1, False, False)
            body(B - 2, 0, False, False)
            body(B - 1, 1, False, True)
            tail(B, 0)

        def p_count(b, first):
            return 3 if first else 4 * b + 2

        def group_before(b, g, first):
            return [(b, g - 1)] if g else [] if first else [(b - 1, NG - 1)]

        def two_before(b, g, first):
            return [(b, g - 2)] if g >= 2 else [] if first else [(b - 1, NG - 2 + g)]

        with nc.Block() as block:
            @block.sync
            def _(sp):
                sp.dma_start(qs_row[:], q_scale.partition_broadcast(P)).then_inc(rows_loaded, 16)
                sp.dma_start(ks_row[:], k_scale.partition_broadcast(P)).then_inc(rows_loaded, 16)
                split.load(sp, 0, 4)
                xt.load(sp, 1, 1)
                split.load(sp, 4)

                def residual(b):
                    sp.dma_start(norm.r[:], rows(x, b)).then_inc(xr_loaded, 16)
                residual(0)
                sp.wait_ge(xt.turned, 2)
                xt.load(sp, 2, 0)

                def body(b, u, more):
                    if more:
                        sp.wait_ge(xt.turned, 2 * b + 4)
                        xt.load(sp, b + 3, 1 - u)
                    if not (ints(b) and b == 0):
                        norm.store(sp, b - 1)
                        sp.wait_ge(norm.stored, 16 * b)
                        residual(b)
                body(0, 0, True)
                with sp.Fori(0, (B - 4) // 2) as i:
                    body(2 * i + 1, 1, True)
                    body(2 * i + 2, 0, True)
                for b in range(B - 3, B):
                    body(b, b % 2, False)
                after.load_x(sp)
                after.load_weights(sp)
                norm.store(sp, B - 1)
                sp.wait_ge(norm.stored, 16 * B)

            @block.gpsimd
            def _(pool):
                pool.memset(mask[:], 0.0).then_inc(mask_zeroed, 1)
                pool.memset(eps1[:], EPS1)
                pool.memset(half2[:], -0.5)
                pool.memset(pos[:], HD1 ** -0.5)
                pool.memset(neg[:], -HD1 ** -0.5)
                for u in range(2):
                    last = pool.memset(kT[u][:], 0.0)
                last.then_inc(set_up, 1)
                pool.wait_ge(mask_zeroed, 1)
                pool.affine_select(out=mask[:], in_=mask[:], compare_op=ALU.is_ge, fill=NEG, base=0,
                                   pattern=[[-1, P]], channel_multiplier=1).then_inc(set_up, 1)
                pool.wait_ge(set_up, 2)

                def rstds(b, u, t):
                    n = T * b + t
                    pool.wait_ge(mv_done, n + 1)
                    wait_from(pool, kn_done, n - 1)
                    pool.tensor_tensor(rstd[:, t, :], mv[:, t, :, 1], eps1[:], ALU.add).then_inc(ve_done, 1)
                    pool.wait_ge(ve_done, n + 1)
                    pool.tensor_tensor(rstd[:, t, :], rstd[:, t, :], half2[:], ALU.pow).then_inc(rstd_done, 1)
                    pool.wait_ge(rstd_done, n + 1)
                    wait_from(pool, e_done, 8 * NG * (b - 1))
                    pool.tensor_tensor(rq[u][:, t:t + 1], rstd[:, t, 0:1], pos[:], ALU.mult)
                    pool.tensor_tensor(nrq[u][:, t:t + 1], rstd[:, t, 0:1], neg[:], ALU.mult).then_inc(rq_done, 1)

                def normalise(b, g):
                    n, i = NG * b + g, g % 2
                    for p, t in ((p0[i], 0), (p1[i], 1)):
                        pool.wait_ge(rs_done, T * n + t + 1)
                        r = rs[i][:, t, :].unsqueeze(2).to_broadcast([P, GH, p.shape[-1]])
                        pool.tensor_tensor(p[:], p[:], r, ALU.mult).then_inc(pn_done, 1)

                def body(b, u, first, last):
                    for g in range(NG):
                        if g == 1 and not last:
                            rstds(b + 1, 1 - u, 0)
                        if g == 2 and not last:
                            rstds(b + 1, 1 - u, 1)
                        normalise(b, g)
                        if g == 0 and not (ints(b) and b < 2):
                            norm.power(pool, b - 2)
                rstds(0, 0, 0)
                rstds(0, 0, 1)

                def tail(b, u):
                    norm.power(pool, b - 2)
                    norm.power(pool, b - 1)
                d_over(pool, body, tail)

            @block.scalar
            def _(act):
                xt.round_hi(act, 0, 0)
                split.round_hi(act, 0, len(split.pieces))

                def keys(b, u, t, base):
                    n = T * b + t
                    act.wait_ge(rstd_done, n + 1)
                    act.wait_ge(p_free[1], base + t + 1)
                    act.activation(kn[t][:], kn[t][:], ACT.Copy, scale=rstd[:, t, 1:2]).then_inc(kn_done, 1)

                def turned_q(b, u, t):
                    act.wait_ge(qk_turned, 4 * b + 2 * t + 1)
                    act.activation(qT[u][:, :, t, :], t_ps[t][:], ACT.Copy).then_inc(t_free[t], 1)

                def values(b, u):
                    for t in range(T):
                        act.wait_ge(p_mm, 6 * b + 4 + t + 1)
                        wait_from(act, pv_mm, NG * (b - 1))
                        act.activation(vt[u][:, t, :], p_ps[t][:], ACT.Copy).then_inc(p_free[t], 1)

                def copy_s10(b, g):
                    n, i = NG * b + g, g % 2
                    act.wait_ge(s_mm, 3 * n + 2)
                    wait_from(act, pt_mm, 3 * (n - 1))
                    act.activation(p1[i][:, :, 0:P], s_ps[1][:], ACT.Copy).then_inc(s_free[1], 1)

                def exps(b, u, g):
                    n, i = NG * b + g, g % 2
                    for t, p in enumerate((p0[i], p1[i])):
                        act.wait_ge(nb_done, T * n + t + 1)
                        for h in range(GH):
                            act.activation(p[:, h, :], p[:, h, :], ACT.Exp, bias=nb[i][:, t, h:h + 1],
                                           scale=rq[u][:, t:t + 1], accum_out=sums[i][:, t, h:h + 1]).then_inc(e_done, 1)

                def copy_pt(b, g, m):
                    n, i = NG * b + g, g % 2
                    act.wait_ge(pt_mm, 3 * n + m + 1)
                    wait_from(act, pv_mm, n - 1)
                    act.activation(pT[i][:, :, m * P:(m + 1) * P], t_ps[(g + m) % 2][:], ACT.Copy)\
                       .then_inc(t_free[(g + m) % 2], 1)

                def round_out(b, u, g):
                    n = NG * b + g
                    act.wait_ge(pv_mm, n + 1)
                    if g == 0:
                        wait_from(act, o_mm, 2 * (b - 1))
                    act.activation(oh[u][:, g, :], v_ps[:], ACT.Copy).then_inc(oh_done, 1)

                def body(b, u, first, last):
                    for g in range(NG):
                        for c, r in two_before(b, g, first):
                            round_out(c, u if g >= 2 else 1 - u, r)
                        copy_s10(b, g)
                        for c, r in group_before(b, g, first):
                            copy_pt(c, r, 0)
                            copy_pt(c, r, 1)
                        if g in (1, 2) and not last:
                            keys(b + 1, 1 - u, g - 1, p_count(b, first))
                        exps(b, u, g)
                        if g in (1, 2) and not last:
                            turned_q(b + 1, 1 - u, g - 1)
                        if g == 2 and not last:
                            values(b + 1, 1 - u)
                        if g in (0, 2) and not last and not (ints(b) and b == B - 2):
                            xt.round_hi(act, b + 2, u, [g // 2])

                keys(0, 0, 0, 0)
                turned_q(0, 0, 0)
                keys(0, 0, 1, 0)
                turned_q(0, 0, 1)
                values(0, 0)
                xt.round_hi(act, 1, 1)

                def tail(b, u):
                    round_out(b - 1, 1 - u, NG - 2)
                    copy_pt(b - 1, NG - 1, 0)
                    copy_pt(b - 1, NG - 1, 1)
                    round_out(b - 1, 1 - u, NG - 1)
                d_over(act, body, tail)

            @block.vector
            def _(dve):
                xt.take_lo(dve, 0, 0)
                split.take_lo(dve, 0, 4)
                dve.wait_ge(rows_loaded, 32)

                def centre(b, u, t):
                    n = T * b + t
                    for i in range(2):
                        dve.wait_ge(p_mm, 6 * b + 2 * t + i + 1)
                        dve.bn_stats(st[:, t, i, :], p_ps[i][:]).then_inc(st_done, 1)
                    wait_from(dve, ve_done, n - 1)
                    dve.wait_ge(st_done, 2 * n + 2)
                    dve.sem_inc(st_seen, 1)
                    for i in range(2):
                        last = dve.bn_aggr(mv[:, t, i, :], st[:, t, i, :])
                    last.then_inc(mv_done, 1)
                    dve.wait_ge(mv_done, n + 1)
                    wait_from(dve, qk_turned, 4 * (b - 1) + 2 * t + 2)
                    for i, (out, row) in enumerate(((qn[t], qs_row), (kn[t], ks_row))):
                        dve.scalar_tensor_tensor(out[:], p_ps[i][:], mv[:, t, i, 0:1], row[:], ALU.subtract, ALU.mult)\
                           .then_inc(p_free[i], 1)

                def turned_k(b, u, t):
                    dve.wait_ge(qk_turned, 4 * b + 2 * t + 2)
                    for h in range(GH):
                        q = slice(h * HD1, (h + 1) * HD1)
                        last = dve.tensor_copy(kT[u][q, :, t, h, :], t_ps[1 - t][q, :, :])
                    last.then_inc(t_free[1 - t], 1)

                def scores(b, u, g):
                    n, i = NG * b + g, g % 2
                    m_ = mask[:].unsqueeze(1).to_broadcast([P, GH, P])
                    for t, p, part in ((0, p0[i], slice(0, P)), (1, p1[i], slice(P, S))):
                        dve.wait_ge(s_mm, 3 * n + 1 + 2 * t)
                        if t == 0:
                            wait_from(dve, pt_mm, 3 * (n - 1))
                        dve.tensor_tensor(p[:, :, part], s_ps[0][:], m_, ALU.add).then_inc(s_free[0], 1)
                        if t == 1:
                            dve.wait_ge(s_free[1], n + 1)
                        dve.wait_ge(s_free[0], 2 * n + t + 1)
                        dve.tensor_reduce(mx[i][:, t, :], p[:], AX.X, ALU.max).then_inc(mx_done, 1)
                        dve.wait_ge(mx_done, T * n + t + 1)
                        if t == 0:
                            dve.wait_ge(rq_done, T * b + T)
                            wait_from(dve, e_done, 8 * (n - 1))
                        dve.tensor_scalar(nb[i][:, t, :], mx[i][:, t, :], nrq[u][:, t:t + 1], None, ALU.mult)\
                           .then_inc(nb_done, 1)

                def reciprocals(b, g):
                    n, i = NG * b + g, g % 2
                    for t in range(T):
                        dve.wait_ge(e_done, 8 * n + 4 * (t + 1))
                        dve.reciprocal(rs[i][:, t, :], sums[i][:, t, :]).then_inc(rs_done, 1)

                def copy_pt(b, g):
                    n, i = NG * b + g, g % 2
                    dve.wait_ge(pt_mm, 3 * n + 3)
                    wait_from(dve, pv_mm, n - 1)
                    dve.tensor_copy(pT[i][:, :, 2 * P:3 * P], t_ps[g % 2][:]).then_inc(t_free[g % 2], 1)

                def lo_out(b, u, g):
                    dve.wait_ge(oh_done, NG * b + g + 1)
                    dve.tensor_tensor(ol[u][:, g, :], v_ps[:], oh[u][:, g, :], ALU.subtract).then_inc(ol_done, 1)

                def residual(b):
                    dve.wait_ge(xr_loaded, 16 * b + 16)
                    for t in range(T):
                        dve.wait_ge(o_mm, T * b + t + 1)
                        dve.tensor_tensor(norm.r[:, t, :], p_ps[t][:], norm.r[:, t, :], ALU.add)\
                           .then_inc(p_free[t], 1)

                def statistics(b, count):
                    norm.statistics(dve, b, [(p_free[t], count) for t in range(T)])

                def body(b, u, first, last):
                    for g in range(NG):
                        for c, r in two_before(b, g, first):
                            lo_out(c, u if g >= 2 else 1 - u, r)
                        scores(b, u, g)
                        for c, r in group_before(b, g, first):
                            copy_pt(c, r)
                        if g == 0 and not (ints(b) and b < 2):
                            statistics(b - 2, p_count(b, False))
                        if g == 1 and not (ints(b) and b < 2):
                            norm.apply(dve, b - 2)
                        reciprocals(b, g)
                        if g in (1, 2) and not last:
                            turned_k(b + 1, 1 - u, g - 1)
                        if g < 2 and not last:
                            centre(b + 1, 1 - u, g)
                        if g in (0, 2) and not last and not (ints(b) and b == B - 2):
                            xt.take_lo(dve, b + 2, u, [g // 2])
                        if g == 3 and not first:
                            residual(b - 1)
                        if g == 3 and last:
                            statistics(b - 1, p_count(b, False) + 1)
                            norm.apply(dve, b - 1)

                centre(0, 0, 0)
                split.take_lo(dve, 4, len(split.pieces))
                centre(0, 0, 1)
                dve.wait_ge(set_up, 2)
                for t in range(T):
                    turned_k(0, 0, t)
                xt.take_lo(dve, 1, 1)

                def tail(b, u):
                    lo_out(b - 1, 1 - u, NG - 2)
                    copy_pt(b - 1, NG - 1)
                    lo_out(b - 1, 1 - u, NG - 1)
                    residual(b - 1)
                    statistics(b - 1, p_count(b - 1, False) + 2)
                    norm.apply(dve, b - 1)
                d_over(dve, body, tail)

            @block.tensor
            def _(pe):
                used = {}

                def bank(kind, sems, i):
                    wait_from(pe, sems[i], used[kind, i])
                    used[kind, i] = used[kind, i] + 1

                def project(b, u, unit):
                    i, t = (unit % 2, unit // 2) if unit < 4 else (2, unit - 4)
                    bank("p", p_free, unit % 2)
                    ts = slice(t * P, (t + 1) * P)
                    for k in range(KT):
                        last = three_pass(pe, p_ps[unit % 2][:], xt.hi[u][:, k, ts], xt.lo[u][:, k, ts],
                                          w[0][:, k, i, :], w[1][:, k, i, :], k == 0, k == KT - 1)
                    last.then_inc(p_mm, 1)

                def output(b, u, t):
                    pe.wait_ge(ol_done, NG * b + NG)
                    bank("p", p_free, t)
                    ts = slice(t * P, (t + 1) * P)
                    for k in range(KT):
                        last = three_pass(pe, p_ps[t][:], oh[u][:, k, ts], ol[u][:, k, ts],
                                          wo[0][:, k, :], wo[1][:, k, :], k == 0, k == KT - 1)
                    last.then_inc(o_mm, 1)

                def turn_q(b, u, t, base):
                    pe.wait_ge(p_free[0], base + t + 1)
                    bank("t", t_free, t)
                    for g in range(NG):
                        last = pe.transpose(t_ps[t][:, g, :], qn[t][:, g * P:(g + 1) * P], core.ident[:])
                    last.then_inc(qk_turned, 1)

                def turn_k(b, u, t):
                    pe.wait_ge(kn_done, T * b + t + 1)
                    bank("t", t_free, 1 - t)
                    for g in range(NG):
                        last = pe.transpose(t_ps[1 - t][:, g, :], kn[t][:, g * P:(g + 1) * P], core.ident[:])
                    last.then_inc(qk_turned, 1)

                def scores(b, u, g):
                    if g == 0:
                        for i in range(2):
                            pe.wait_ge(t_free[i], used["t", i])
                    for m in (0, 1):
                        wait_from(pe, s_free[m], (2 - m) * (NG * b + g))
                        pe.matmul(s_ps[m][:], qT[u][:, g, m, :], kT[u][:, g, 0, :, :],
                                  start=True, stop=True).then_inc(s_mm, 1)

                def last_scores(b, u, g):
                    pe.wait_ge(s_free[0], 2 * (NG * b + g) + 1)
                    pe.matmul(s_ps[0][:], qT[u][:, g, 1, :], kT[u][:, g, 1, :, :],
                              start=True, stop=True).then_inc(s_mm, 1)

                def turn_p(b, g):
                    n, i = NG * b + g, g % 2
                    for m in range(3):
                        if m < T:
                            pe.wait_ge(pn_done, T * n + m + 1)
                        bank("t", t_free, (g + m) % 2)
                        for h in range(GH):
                            src = p0[i][:, h, :] if m == 0 else p1[i][:, h, (m - 1) * P:m * P]
                            last = pe.transpose(t_ps[(g + m) % 2][:, h, :], src, core.ident[:])
                        last.then_inc(pt_mm, 1)

                def values(b, u, g):
                    n, i = NG * b + g, g % 2
                    wait_from(pe, ol_done, n)
                    pe.wait_ge(t_free[g % 2], used["t", g % 2])
                    pe.wait_ge(t_free[1 - g % 2], used["t", 1 - g % 2])
                    for tt, cols, src in ((0, slice(0, S), slice(0, S)), (1, slice(P, S), slice(S, S + P))):
                        for h in range(GH):
                            e = (g * GH + h) * HD1
                            last = pe.matmul(v_ps[h * HD1:(h + 1) * HD1, cols], vt[u][:, tt, e:e + HD1],
                                             pT[i][:, h, src], start=(tt == 0), stop=(tt == 1), skip_group_check=True,
                                             tile_position=(0, h * HD1))
                    last.then_inc(pv_mm, 1)

                def body(b, u, first, last):
                    for i in range(2):
                        used["p", i] = p_count(b, first)
                        used["t", i] = 2 if first else 8 * b + 1 - i
                    if not last:
                        xt.wait_ready(pe, b + 1)
                    for g in range(NG):
                        scores(b, u, g)
                        for c, r in group_before(b, g, first):
                            turn_p(c, r)
                        last_scores(b, u, g)
                        if g == 3 and not first:
                            output(b - 1, 1 - u, 0)
                        elif g < 3 and not last:
                            project(b + 1, 1 - u, 2 * g)
                        if g in (1, 2) and not last:
                            turn_q(b + 1, 1 - u, g - 1, p_count(b, first))
                            turn_k(b + 1, 1 - u, g - 1)
                        if g == 3 and not first:
                            output(b - 1, 1 - u, 1)
                        elif g < 3 and not last:
                            project(b + 1, 1 - u, 2 * g + 1)
                        if g == 1:
                            for i in range(2):
                                pe.wait_ge(p_free[i], p_count(b, first))
                        for c, r in group_before(b, g, first):
                            values(c, u if g else 1 - u, r)
                        if g in (0, 2) and not last and not (ints(b) and b == B - 2):
                            xt.turn(pe, b + 2, u, [g // 2])

                xt.turn(pe, 0, 0)
                for i in range(2):
                    used["p", i] = used["t", i] = 0
                xt.wait_ready(pe, 0)
                for unit in range(6):
                    pe.wait_ge(split.lo_done, (2, 4, 4, 4, 6, 6)[unit])
                    project(0, 0, unit)
                pe.wait_ge(split.lo_done, len(split.pieces))
                for t in range(T):
                    turn_q(0, 0, t, 0)
                    turn_k(0, 0, t)
                xt.turn(pe, 1, 1)

                def tail(b, u):
                    turn_p(b - 1, NG - 1)
                    values(b - 1, 1 - u, NG - 1)
                    for t in range(T):
                        output(b - 1, 1 - u, t)
                d_over(pe, body, tail)


HX, CX = S // 32, 32
HT = P // CX
XSCALE = CX ** -0.5
NQ = D // P
STEPS = HX * NQ // 2
HALF = STEPS // 2


def l1_cross(core, ahead, after, x, ctx_in, y, gamma):
    nc = core.nc
    with ExitStack() as ctx:
        sb = lambda n, s, dt=F32: ctx.enter_context(nc.sbuf_tensor(n, s, dt))
        pb = lambda n, s: ctx.enter_context(nc.psum_tensor(n, s, F32))
        norm = Norm(core, ctx, "n5", y)
        xs = [core.x0, sb("e_x1", [P, T, D])]
        xr = [sb(f"e_xr{u}", [P, T, D]) for u in range(2)]
        cs = [ahead.buf(0), sb("e_c1", [P, T, D])]
        parts = {n: sb(f"e_{n}", [P, T, D], F32R) for n in ("xh", "xl", "ch", "cl")}
        qs = [sb(f"qs{u}", [P, T, HT, D], F32R) for u in range(2)]
        ks = [sb(f"ks{u}", [P, T, HT, D], F32R) for u in range(2)]
        vt = [sb(f"e_vt{u}", [P, LB, S]) for u in range(2)]
        pr = [sb(f"e_p{i}", [P, 2, D]) for i in range(2)]
        pT = [sb(f"e_pT{i}", [P, HT, LB, D]) for i in range(2)]
        nb = [sb(f"e_nb{i}", [P, 2]) for i in range(2)]
        sums = [sb(f"e_sums{i}", [P, HT, NQ]) for i in range(2)]
        rs = [sb(f"e_rs{i}", [P, HT, NQ]) for i in range(2)]
        rb = sb("e_rb", [P, D])
        gcol = sb("e_gamma", [P, 1])
        scale = sb("e_scale", [P, T])
        s_ps = [pb(f"e_s_ps{i}", [P, 2, D]) for i in range(2)]
        t_ps = [pb(f"e_t_ps{i}", [P, LB, P]) for i in range(2)]
        v_ps = pb("e_v_ps", [P, D])
        m_ps = pb("e_m_ps", [P, D])

        s = lambda n: core.sem("e_" + n)
        x_loaded, c_loaded, g_loaded = [ahead.x_loaded, s("x1")], [ahead.loaded[0], s("c1")], s("g_loaded")
        xh_done, xl_done, ch_done, cl_done = s("xh_done"), s("xl_done"), s("ch_done"), s("cl_done")
        stacked = [s(f"stacked{j}") for j in range(HT)]
        r_loaded, o_scaled = [s("r_loaded0"), s("r_loaded1")], s("o_scaled")
        scale_set, x_scaled = s("scale_set"), s("x_scaled")
        c_turned, m_read, s_mm, nb_done, e_done = (s(n) for n in (
            "c_turned", "m_read", "s_mm", "nb_done", "e_done"))
        t_mm, ta_done, td_done, rs_done, r_mm, v_mm, o_done = (s(n) for n in (
            "t_mm", "ta_done", "td_done", "rs_done", "r_mm", "v_mm", "o_done"))
        NSTACK = 2 * 4

        PARTS = HALF - 1
        per_part = [LB * HT // PARTS + (k < LB * HT % PARTS) for k in range(PARTS)]

        def before(b, m, first):
            return [(b, m - 2)] if m >= 2 else [] if first else [(b - 1, STEPS - 2 + m)]

        def tile_turned(b, m, first):
            return [(b, 0)] if m == HALF + 2 else [(b - 1, 1)] if m == 2 and not first else []

        def value_part(b, m, first):
            if m >= HALF + 2:
                return [(b, True, 0, m - HALF - 2)]
            if first or m == 1 or m > HALF:
                return []
            return [(b - 1, False, 0, PARTS - 1)] if m == 0 else [(b - 1, False, 1, m - 2)]

        def m_count(b, t):
            return 4 * b + (3 if t == 0 else 4 if ints(b) and b == B - 1 else 6)

        def in_buffer(eng, sems, b, u):
            eng.wait_ge(sems[u], 16 * (b // 2) + 16 if ints(b) else 8 * (b - u) + 16)

        def take_lo(eng, b, u, n):
            hi, done, lo, src, mine = (("xh", xh_done, "xl", xs, xl_done) if n == "xl"
                                       else ("ch", ch_done, "cl", cs, cl_done))
            eng.wait_ge(done, b + 1)
            eng.tensor_tensor(parts[lo][:], src[u][:], parts[hi][:], ALU.subtract).then_inc(mine, 1)

        with nc.Block() as block:
            @block.sync
            def _(sp):
                sp.dma_start(gcol[:], gamma.partition_broadcast(P)).then_inc(g_loaded, 16)

                def load(b, u):
                    sp.dma_start(xs[u][:], rows(x, b)).then_inc(x_loaded[u], 16)
                    sp.dma_start(cs[u][:], rows(ctx_in, b)).then_inc(c_loaded[u], 16)

                def stack(b, u):
                    sp.wait_ge(xl_done, b + 1)
                    sp.wait_ge(cl_done, b + 1)
                    for j in range(HT):
                        for dst, hi, lo, plan in ((qs, "xh", "xl", "hlhl"), (ks, "ch", "cl", "hhll")):
                            for r, part in enumerate(plan):
                                src = parts[hi if part == "h" else lo]
                                sp.dma_start(dst[u][r * CX:(r + 1) * CX, :, j, :].bitcast(F32),
                                             src[j * CX:(j + 1) * CX, :, :].bitcast(F32)).then_inc(stacked[j], 16)

                def residual(b, u):
                    wait_from(sp, o_done, T * (b - 1))
                    sp.dma_start(xr[u][:], rows(x, b)).then_inc(r_loaded[u], 16)

                load(1, 1)
                stack(0, 0)
                residual(0, 0)
                sp.wait_ge(c_turned, 2)
                load(2, 0)

                def body(b, u, more):
                    if not (ints(b) and b == B - 1):
                        stack(b + 1, 1 - u)
                    if more:
                        sp.wait_ge(c_turned, 2 * b + 4)
                        load(b + 3, 1 - u)
                    if not (ints(b) and b == B - 1):
                        residual(b + 1, 1 - u)
                    if not (ints(b) and b == 0):
                        norm.store(sp, b - 1)
                body(0, 0, True)
                with sp.Fori(0, (B - 4) // 2) as i:
                    body(2 * i + 1, 1, True)
                    body(2 * i + 2, 0, True)
                for b in range(B - 3, B):
                    body(b, b % 2, False)
                after.load_x(sp)
                norm.store(sp, B - 1)
                sp.wait_ge(norm.stored, 16 * B)

            @block.gpsimd
            def _(pool):
                def scale_x(b, u):
                    in_buffer(pool, x_loaded, b, u)
                    pool.tensor_tensor(xs[u][:], xs[u][:], scale[:].unsqueeze(2).to_broadcast([P, T, D]), ALU.mult)\
                        .then_inc(x_scaled, 1)

                def body(b, u, first, last):
                    if not last:
                        scale_x(b + 1, 1 - u)
                        take_lo(pool, b + 1, 1 - u, "cl")
                        take_lo(pool, b + 1, 1 - u, "xl")
                    if not first:
                        norm.power(pool, b - 1)

                pool.memset(scale[:], XSCALE).then_inc(scale_set, 1)
                pool.wait_ge(scale_set, 1)
                scale_x(0, 0)
                take_lo(pool, 0, 0, "xl")
                over_batches(pool, body, lambda b, u: norm.power(pool, b - 1))

            @block.scalar
            def _(act):
                act.wait_ge(g_loaded, 16)

                def round_hi(b, u, n):
                    loaded, done, src = (x_loaded, xh_done, xs) if n == "xh" else (c_loaded, ch_done, cs)
                    if n == "xh":
                        act.wait_ge(x_scaled, b + 1)
                    else:
                        in_buffer(act, loaded, b, u)
                    for j in range(HT):
                        wait_from(act, stacked[j], 16 * NSTACK * b)
                    act.activation(parts[n][:], src[u][:], ACT.Copy).then_inc(done, 1)

                def context(b, u, r):
                    act.wait_ge(c_turned, 2 * b + r + 1)
                    wait_from(act, v_mm, T * (b - 1))
                    act.activation(vt[u][:, 2 * r:2 * r + 2, :].rearrange("p k s -> p (k s)"), m_ps[:], ACT.Copy)\
                       .then_inc(m_read, 1)

                def exps(b, m):
                    n, i, j = STEPS * b + m, m % 2, m // 2 % HT
                    t = m // (HALF)
                    act.wait_ge(nb_done, n + 1)
                    wait_from(act, t_mm, 2 * (n - 1))
                    if m % (HALF) == 0:
                        wait_from(act, rs_done, T * b + t - 1)
                    for a in range(2):
                        q = 2 * (m % 2) + a
                        act.activation(pr[i][:, a, :], s_ps[i][:, a, :], ACT.Exp, bias=nb[i][:, a:a + 1],
                                       accum_out=sums[t][:, j, q:q + 1]).then_inc(e_done, 1)

                def copy_t(b, m):
                    n, j, q = STEPS * b + m, m // 2 % HT, 2 * (m % 2)
                    t = m // (HALF)
                    act.wait_ge(t_mm, 2 * n + 1)
                    wait_from(act, v_mm, T * b + t - 1)
                    act.activation(pT[t][:, j, :, q * P:(q + 1) * P], t_ps[0][:], ACT.Copy).then_inc(ta_done, 1)

                def spread(b, t):
                    act.wait_ge(r_mm, T * b + t + 1)
                    wait_from(act, o_done, T * b + t)
                    act.activation(rb[:], m_ps[:], ACT.Copy, scale=gcol[:]).then_inc(m_read, 1)

                def body(b, u, first, last):
                    for m in range(STEPS):
                        for c, r in before(b, m, first):
                            copy_t(c, r)
                        exps(b, m)
                        for c, t in tile_turned(b, m - 1, first):
                            spread(c, t)
                        if not last:
                            if m == (3 if first else 0):
                                round_hi(b + 1, 1 - u, "ch")
                            if m == (4 if first else 1):
                                round_hi(b + 1, 1 - u, "xh")
                            if m in (HALF + 4, HALF + 6):
                                context(b + 1, 1 - u, (m - HALF - 4) // 2)

                round_hi(0, 0, "ch")
                round_hi(0, 0, "xh")
                context(0, 0, 0)
                context(0, 0, 1)

                def tail(b, u):
                    copy_t(b - 1, STEPS - 2)
                    copy_t(b - 1, STEPS - 1)
                    spread(b - 1, 1)
                over_batches(act, body, tail)

            @block.vector
            def _(dve):
                def maxima(b, m):
                    n, i = STEPS * b + m, m % 2
                    dve.wait_ge(s_mm, n + 1)
                    wait_from(dve, e_done, 2 * (n - 1))
                    dve.tensor_reduce(nb[i][:], s_ps[i][:], AX.X, ALU.max, negate=True).then_inc(nb_done, 1)

                def copy_t(b, m):
                    n, j, q = STEPS * b + m, m // 2 % HT, 2 * (m % 2) + 1
                    t = m // (HALF)
                    dve.wait_ge(t_mm, 2 * n + 2)
                    wait_from(dve, v_mm, T * b + t - 1)
                    dve.tensor_copy(pT[t][:, j, :, q * P:(q + 1) * P], t_ps[1][:]).then_inc(td_done, 1)

                def reciprocals(b, t):
                    dve.wait_ge(e_done, 2 * (STEPS * b + HALF * (t + 1)))
                    wait_from(dve, r_mm, T * b + t - 1)
                    dve.reciprocal(rs[t][:], sums[t][:]).then_inc(rs_done, 1)

                def scale_out(b, u, t):
                    dve.wait_ge(v_mm, T * b + t + 1)
                    dve.wait_ge(m_read, m_count(b, t))
                    dve.tensor_tensor(rb[:], v_ps[:], rb[:], ALU.mult).then_inc(o_scaled, 1)
                    dve.wait_ge(o_scaled, T * b + t + 1)
                    if t == 0:
                        in_buffer(dve, r_loaded, b, u)
                        norm.wait_stored(dve, b)
                    dve.tensor_tensor(norm.r[:, t, :], xr[u][:, t, :], rb[:], ALU.add).then_inc(o_done, 1)

                def finish(b, u):
                    norm.statistics(dve, b, [(o_done, T * b + t + 1) for t in range(T)])

                def body(b, u, first, last):
                    for m in range(STEPS):
                        maxima(b, m)
                        for c, r in before(b, m, first):
                            copy_t(c, r)
                            if r == STEPS - 1 or r == HALF - 1:
                                reciprocals(c, r // (HALF))
                        if m in (1, HALF + 1) and not first:
                            scale_out(b - 1, 1 - u, m // HALF)
                        if m == HALF + 2 and not first:
                            finish(b - 1, 1 - u)
                        if m == HALF + 4 and not first:
                            norm.apply(dve, b - 1)

                def tail(b, u):
                    copy_t(b - 1, STEPS - 2)
                    scale_out(b - 1, 1 - u, 0)
                    copy_t(b - 1, STEPS - 1)
                    reciprocals(b - 1, 1)
                    scale_out(b - 1, 1 - u, 1)
                    finish(b - 1, 1 - u)
                    norm.apply(dve, b - 1)
                take_lo(dve, 0, 0, "cl")
                over_batches(dve, body, tail)

            @block.tensor
            def _(pe):
                used = [0]

                def m_bank():
                    wait_from(pe, m_read, used[0])
                    used[0] = used[0] + 1

                def turn_context(b, u, r):
                    in_buffer(pe, c_loaded, b, u)
                    m_bank()
                    for k in range(2):
                        for t in range(T):
                            cols = slice((2 * r + k) * P, (2 * r + k + 1) * P)
                            last = pe.transpose(m_ps[:, (k * T + t) * P:(k * T + t + 1) * P], cs[u][:, t, cols],
                                                core.ident[:])
                    last.then_inc(c_turned, 1)

                def scores(b, u, m):
                    n, i, h = STEPS * b + m, m % 2, m // 2
                    wait_from(pe, e_done, 2 * (n - 1))
                    for a in range(2):
                        q = 2 * (m % 2) + a
                        last = pe.matmul(s_ps[i][:, a, :], qs[u][:, h // HT, h % HT, q * P:(q + 1) * P],
                                         ks[u][:, h // HT, h % HT, :], start=True, stop=True)
                    last.then_inc(s_mm, 1)

                def turn(b, m):
                    n = STEPS * b + m
                    for a, read in ((0, ta_done), (1, td_done)):
                        pe.wait_ge(e_done, 2 * n + 1 + a)
                        wait_from(pe, read, n)
                        for k in range(LB):
                            last = pe.transpose(t_ps[a][:, k, :], pr[m % 2][:, a, k * P:(k + 1) * P], core.ident[:])
                        last.then_inc(t_mm, 1)

                def spread_sums(b, t):
                    pe.wait_ge(rs_done, T * b + t + 1)
                    m_bank()
                    for q in range(NQ):
                        for j in range(HT):
                            last = pe.matmul(m_ps[j * CX:(j + 1) * CX, q * P:(q + 1) * P],
                                             rs[t][:, j, q:q + 1].to_broadcast([P, CX]), core.ident[:],
                                             start=True, stop=True, skip_group_check=True, tile_position=(0, j * CX))
                    last.then_inc(r_mm, 1)

                def values(b, u, t, part):
                    if part == 0:
                        n = STEPS * b + HALF * (t + 1)
                        pe.wait_ge(ta_done, n)
                        pe.wait_ge(td_done, n)
                        wait_from(pe, o_done, T * b + t)
                    start = sum(per_part[:part])
                    for k, j in [divmod(n, HT) for n in range(start, start + per_part[part])]:
                        e = t * P + j * CX
                        last = pe.matmul(v_ps[j * CX:(j + 1) * CX, :], vt[u][:, k, e:e + CX], pT[t][:, j, k, :],
                                         start=(k == 0), stop=(k == LB - 1), skip_group_check=True,
                                         tile_position=(0, j * CX))
                    if part == PARTS - 1:
                        last.then_inc(v_mm, 1)

                def body(b, u, first, last):
                    used[0] = 2 if first else 4 * b + 1
                    for m in range(STEPS):
                        if m % 2 == 0 and m < 2 * HT:
                            pe.wait_ge(stacked[m // 2], 16 * NSTACK * (b + 1))
                        scores(b, u, m)
                        for c, r in before(b, m, first):
                            turn(c, r)
                        for c, t in tile_turned(b, m, first):
                            spread_sums(c, t)
                        for c, own, t, part in value_part(b, m, first):
                            values(c, u if own else 1 - u, t, part)
                        if m in (HALF + 4, HALF + 6) and not last:
                            turn_context(b + 1, 1 - u, (m - HALF - 4) // 2)

                turn_context(0, 0, 0)
                turn_context(0, 0, 1)

                def tail(b, u):
                    values(b - 1, 1 - u, 0, PARTS - 1)
                    turn(b - 1, STEPS - 2)
                    turn(b - 1, STEPS - 1)
                    spread_sums(b - 1, 1)
                    for part in range(PARTS):
                        values(b - 1, 1 - u, 1, part)
                over_batches(pe, body, tail)


E, R, TOPK = 8, 16, 2
BONUS = 3.0 * (1.0 - min(1 / 1250, 1.0))


def l1_experts(core, ahead, x, y, wr, br, wdn, bd, wup, bu):
    nc = core.nc
    with ExitStack() as ctx:
        sb = lambda n, s, dt=F32: ctx.enter_context(nc.sbuf_tensor(n, s, dt))
        pb = lambda n, s: ctx.enter_context(nc.psum_tensor(n, s, F32))
        norm = Norm(core, ctx, "n6", y)
        wrd = sb("wrd", [P, KT, E + E * R])
        wu, bup = sb("f_wu", [P, D]), sb("f_bu", [P, D])
        bias = sb("f_bias", [P, 1, E + E * R])
        numbers = sb("f_numbers", [P, 1, 1, E])
        xs = [core.x0, sb("f_x1", [P, T, D])]
        xr = [sb(f"f_xr{u}", [P, T, D]) for u in range(2)]
        xT = [sb(f"f_xT{u}", [P, KT, S]) for u in range(2)]
        lh = sb("f_lh", [P, T, E + E * R])
        largest = sb("f_largest", [P, T])
        ex, gates = sb("f_ex", [P, T, E]), sb("f_gates", [P, T, E])
        den, rden = sb("f_den", [P, T]), sb("f_rden", [P, T])
        top = sb("f_top", [P, T, 8])
        index = sb("f_index", [P, T, 8], mybir.dt.uint32)
        chosen = sb("f_chosen", [P, T, TOPK])
        tsum, share = sb("f_tsum", [P, T]), sb("f_share", [P, T, TOPK])
        pick = sb("f_pick", [P, T, TOPK, E])
        w = sb("f_w", [P, T, P])
        hw = sb("f_hw", [P, T, E * R])
        hwT, wT = sb("f_hwT", [P, S]), sb("f_wT", [P, S])
        x_ps = [pb(f"f_x_ps{r}", [P, 2, S]) for r in range(2)]
        h_ps = [pb(f"f_h_ps{u}", [P, T, E + E * R]) for u in range(2)]
        t_ps = pb("f_t_ps", [P, 2, S])
        o_ps = [pb(f"f_o_ps{t}", [P, D]) for t in range(T)]

        s = lambda n: core.sem("f_" + n)
        x_loaded, xr_loaded = [ahead.x_loaded, s("x1")], [s("xr0"), s("xr1")]
        w_loaded, up_loaded, prepared, zeroed = s("w_loaded"), s("up_loaded"), s("prepared"), s("zeroed")
        x_turned, xT_done, h_mm, shifted, e_done = s("x_turned"), s("xT_done"), s("h_mm"), s("shifted"), s("e_done")
        hw_done, h_turned, hT_done, o_mm = s("hw_done"), s("h_turned"), s("hT_done"), s("o_mm")
        lh_done, largest_done = s("lh_done"), s("largest_done")
        den_done, gates_done, carried = s("den_done"), s("gates_done"), s("carried")
        top_done, index_done, chosen_done = s("top_done"), s("index_done"), s("chosen_done")
        tsum_done, share_done, pick_done, w_done = s("tsum_done"), s("share_done"), s("pick_done"), s("w_done")

        with nc.Block() as block:
            @block.sync
            def _(sp):
                def load(b, u):
                    sp.dma_start(xs[u][:], rows(x, b)).then_inc(x_loaded[u], 16)

                def residual(b, u):
                    sp.dma_start(xr[u][:], rows(x, b)).then_inc(xr_loaded[u], 16)
                with nc.allow_non_contiguous_dma(reason="rows of 8 router weights, once"):
                    sp.dma_start(wrd[:, :, 0:E], wr.rearrange("(k p) n -> p k n", p=P)).then_inc(w_loaded, 16)
                sp.dma_start(wrd[:, :, E:], wdn.rearrange("(k p) n -> p k n", p=P)).then_inc(w_loaded, 16)
                sp.dma_start(bias[:, 0, 0:E], br.partition_broadcast(P)).then_inc(w_loaded, 16)
                sp.dma_start(bias[:, 0, E:], bd.partition_broadcast(P)).then_inc(w_loaded, 16)
                load(1, 1)
                sp.dma_start(wu[:], wup).then_inc(up_loaded, 16)
                sp.wait_ge(zeroed, 1)
                sp.dma_start(bup[0:E, :], bu).then_inc(up_loaded, 16)
                residual(0, 0)
                residual(1, 1)
                sp.wait_ge(x_turned, 2)
                load(2, 0)

                def body(b, u, more):
                    if more:
                        sp.wait_ge(x_turned, 2 * b + 4)
                        load(b + 3, 1 - u)
                    if not (ints(b) and b == 0):
                        norm.store(sp, b - 1)
                        if not (ints(b) and b == B - 1):
                            residual(b + 1, 1 - u)
                body(0, 0, True)
                with sp.Fori(0, (B - 4) // 2) as i:
                    body(2 * i + 1, 1, True)
                    body(2 * i + 2, 0, True)
                for b in range(B - 3, B):
                    body(b, b % 2, False)
                norm.store(sp, B - 1)
                sp.wait_ge(norm.stored, 16 * B)

            @block.gpsimd
            def _(pool):
                pool.memset(w[:], 0.0).then_inc(prepared, 1)
                pool.memset(bup[:], 0.0).then_inc(zeroed, 1)
                pool.iota(numbers[:, 0, 0, :], pattern=[[1, E]], base=0, channel_multiplier=0,
                          allow_small_or_imprecise_dtypes=True).then_inc(prepared, 1)
                over_batches(pool, lambda b, u, first, last: norm.power(pool, b))

            @block.scalar
            def _(act):
                def turned(b, u):
                    for r in range(2):
                        act.wait_ge(x_turned, 2 * b + r + 1)
                        wait_from(act, h_mm, b - 1)
                        act.activation(xT[u][:, 2 * r:2 * r + 2, :], x_ps[r][:], ACT.Copy).then_inc(xT_done, 1)

                def exponential(b):
                    act.wait_ge(shifted, b + 1)
                    wait_from(act, gates_done, b)
                    act.activation(ex[:], lh[:, :, 0:E], ACT.Exp).then_inc(e_done, 1)

                def hidden(b, u):
                    act.wait_ge(h_turned, b + 1)
                    wait_from(act, o_mm, T * b)
                    act.activation(hwT[:], t_ps[:, 0, :], ACT.Copy).then_inc(hT_done, 1)
                    act.activation(wT[:], t_ps[:, 1, :], ACT.Copy).then_inc(hT_done, 1)

                def body(b, u, first, last):
                    if not last:
                        turned(b + 1, 1 - u)
                    if not first:
                        hidden(b - 1, 1 - u)
                    exponential(b)
                turned(0, 0)
                over_batches(act, body, lambda b, u: hidden(b - 1, 1 - u))

            @block.vector
            def _(dve):
                def shift(b, u):
                    dve.wait_ge(h_mm, b + 1)
                    wait_from(dve, hw_done, T * b)
                    dve.tensor_tensor(lh[:], h_ps[u][:], bias[:].to_broadcast([P, T, E + E * R]),
                                      ALU.add).then_inc(lh_done, 1)
                    dve.wait_ge(lh_done, b + 1)
                    dve.tensor_reduce(largest[:], lh[:, :, 0:E], AX.X, ALU.max).then_inc(largest_done, 1)
                    dve.wait_ge(largest_done, b + 1)
                    dve.tensor_tensor(lh[:, :, 0:E], lh[:, :, 0:E], largest[:].unsqueeze(2).to_broadcast([P, T, E]),
                                      ALU.subtract).then_inc(shifted, 1)

                def route(b):
                    dve.wait_ge(e_done, b + 1)
                    dve.tensor_reduce(den[:], ex[:], AX.X, ALU.add).then_inc(den_done, 1)
                    dve.wait_ge(den_done, 2 * b + 1)
                    dve.reciprocal(rden[:], den[:]).then_inc(den_done, 1)
                    dve.wait_ge(den_done, 2 * b + 2)
                    dve.tensor_tensor(gates[:], ex[:], rden[:].unsqueeze(2).to_broadcast([P, T, E]),
                                      ALU.mult).then_inc(gates_done, 1)
                    dve.wait_ge(gates_done, b + 1)
                    dve.sem_inc(carried, 1)
                    for t in range(T):
                        dve.max(top[:, t, :], gates[:, t, :]).then_inc(top_done, 1)
                    dve.wait_ge(top_done, T * b + T)
                    dve.sem_inc(carried, 1)
                    for t in range(T):
                        dve.max_index(index[:, t, :], top[:, t, :], gates[:, t, :]).then_inc(index_done, 1)
                    dve.tensor_tensor(tsum[:], top[:, :, 0], top[:, :, 1], ALU.add).then_inc(tsum_done, 1)
                    dve.wait_ge(index_done, T * b + T)
                    dve.tensor_copy(chosen[:], index[:, :, 0:TOPK]).then_inc(chosen_done, 1)
                    dve.wait_ge(tsum_done, 2 * b + 1)
                    dve.reciprocal(tsum[:], tsum[:]).then_inc(tsum_done, 1)
                    dve.wait_ge(chosen_done, b + 1)
                    dve.tensor_tensor(pick[:], numbers[:].to_broadcast([P, T, TOPK, E]),
                                      chosen[:].unsqueeze(3).to_broadcast([P, T, TOPK, E]),
                                      ALU.is_equal).then_inc(pick_done, 1)
                    dve.wait_ge(tsum_done, 2 * b + 2)
                    dve.tensor_tensor(share[:], top[:, :, 0:TOPK], tsum[:].unsqueeze(2).to_broadcast([P, T, TOPK]),
                                      ALU.mult).then_inc(share_done, 1)
                    dve.wait_ge(pick_done, 2 * b + 1)
                    dve.wait_ge(share_done, b + 1)
                    dve.tensor_tensor(pick[:], pick[:], share[:].unsqueeze(3).to_broadcast([P, T, TOPK, E]),
                                      ALU.mult).then_inc(pick_done, 1)
                    dve.wait_ge(pick_done, 2 * b + 2)
                    wait_from(dve, h_turned, b)
                    dve.tensor_tensor(w[:, :, 0:E], pick[:, :, 0, :], pick[:, :, 1, :], ALU.add).then_inc(w_done, 1)
                    dve.wait_ge(w_done, b + 1)
                    for t in range(T):
                        dve.scalar_tensor_tensor(hw[:, t, :].rearrange("p (e r) -> p e r", r=R),
                                                 lh[:, t, E:].rearrange("p (e r) -> p e r", r=R), 0.0,
                                                 w[:, t, 0:E].unsqueeze(2).to_broadcast([P, E, R]),
                                                 ALU.max, ALU.mult).then_inc(hw_done, 1)

                def residual(b, u):
                    for t in range(T):
                        dve.wait_ge(o_mm, T * b + t + 1)
                        if t == 0:
                            dve.wait_ge(xr_loaded[u], 16 * (b // 2) + 16 if ints(b) else 8 * (b - u) + 16)
                            norm.wait_stored(dve, b)
                        dve.tensor_tensor(norm.r[:, t, :], o_ps[t][:], xr[u][:, t, :], ALU.add).then_inc(norm.added, 1)
                    norm.statistics(dve, b)

                def body(b, u, first, second):
                    shift(b, u)
                    if not first and not second:
                        norm.apply(dve, b - 2)
                    route(b)
                    if not first:
                        residual(b - 1, 1 - u)

                dve.wait_ge(w_loaded, 64)
                dve.tensor_scalar(bias[:, 0, 0:E], bias[:, 0, 0:E], BONUS, None, ALU.add).then_inc(prepared, 1)
                dve.wait_ge(prepared, 3)

                def tail(b, u):
                    norm.apply(dve, b - 2)
                    residual(b - 1, 1 - u)
                    norm.apply(dve, b - 1)
                body(0, 0, True, False)
                body(1, 1, False, True)
                with dve.Fori(0, (B - 2) // 2) as i:
                    body(2 * i + 2, 0, False, False)
                    body(2 * i + 3, 1, False, False)
                tail(B, 0)

            @block.tensor
            def _(pe):
                def turn_x(b, u):
                    pe.wait_ge(x_loaded[u], 16 * (b // 2) + 16 if ints(b) else 8 * (b - u) + 16)
                    for r in range(2):
                        wait_from(pe, xT_done, 2 * (b - 1) + r + 1)
                        for k in range(2):
                            for t in range(T):
                                kt = 2 * r + k
                                last = pe.transpose(x_ps[r][:, k, t * P:(t + 1) * P],
                                                    xs[u][:, t, kt * P:(kt + 1) * P], core.ident[:])
                        last.then_inc(x_turned, 1)

                def project(b, u):
                    pe.wait_ge(xT_done, 2 * b + 2)
                    wait_from(pe, lh_done, b - 1)
                    for t in range(T):
                        for k in range(KT):
                            last = pe.matmul(h_ps[u][:, t, :], xT[u][:, k, t * P:(t + 1) * P], wrd[:, k, :],
                                             start=(k == 0), stop=(k == KT - 1), skip_group_check=True)
                    last.then_inc(h_mm, 1)

                def turn_hidden(b):
                    pe.wait_ge(hw_done, T * b + T)
                    wait_from(pe, hT_done, 2 * b)
                    for t in range(T):
                        pe.transpose(t_ps[:, 0, t * P:(t + 1) * P], hw[:, t, :], core.ident[:])
                        last = pe.transpose(t_ps[:, 1, t * P:(t + 1) * P], w[:, t, :], core.ident[:])
                    last.then_inc(h_turned, 1)

                def out(b, u):
                    pe.wait_ge(hT_done, 2 * b + 2)
                    for t in range(T):
                        if t == 0:
                            wait_from(pe, norm.added, T * b)
                        pe.matmul(o_ps[t][:], hwT[:, t * P:(t + 1) * P], wu[:], start=True, stop=False)
                        pe.matmul(o_ps[t][:], wT[:, t * P:(t + 1) * P], bup[:],
                                  start=False, stop=True).then_inc(o_mm, 1)

                def body(b, u, first, last):
                    if not last:
                        turn_x(b + 1, 1 - u)
                    if not first:
                        turn_hidden(b - 1)
                    if not last:
                        project(b + 1, 1 - u)
                    if not first:
                        out(b - 1, 1 - u)

                turn_x(0, 0)
                pe.wait_ge(w_loaded, 64)
                project(0, 0)
                pe.wait_ge(up_loaded, 32)

                def tail(b, u):
                    turn_hidden(b - 1)
                    out(b - 1, 1 - u)
                over_batches(pe, body, tail)


def decoder(nc, x, ctx, ctx_rev, wqT, bq, wkT, bk, wvT, bv, woT, ssm_kernel, d_skip, gateT, upT, downT, gate_s,
            up_s, down_s, wqkv, q_scale, k_scale, wout, gamma, wr, br, wdn, bd, wup, bu, out):
    with ExitStack() as stack:
        core = Core(nc, stack)
        between = [nc.dram_tensor(f"x_after_{i}", (B * S, D), F32, kind="Internal").ap() for i in range(1, 6)]
        padded = nc.dram_tensor("padded_kernels", (HC, PAD + D), F32, kind="Internal").ap()
        to_kv = Ahead(core, "a1", x, kv_weights(wkT, wvT), 2 * D)
        to_attention = Ahead(core, "a2", x, qo_weights(wqT, woT), 2 * D)
        to_convolution = Ahead(core, "b", between[0], [rows(ctx_rev, 0)], 2 * D)
        to_feed_forward = Ahead(core, "c", between[1], ffn_weights(gateT, upT, downT), D)
        to_causal = Ahead(core, "d", between[2], qkvo_weights(wqkv, wout), 2 * D)
        to_cross = Ahead(core, "e", between[3], [rows(ctx, 0)], 2 * D)
        to_experts = Ahead(core, "f", between[4])
        constants(core, to_kv)
        with nc.sbuf_tensor("kv", [P, B, KVH, HD + 1], F32) as kv:
            l0_keys_values(core, to_kv, to_attention, kv, x, bk, bv)
            l0_attention(core, to_attention, to_convolution, kv, x, between[0], bq)
        core.clear()
        l0_convolution(core, to_convolution, to_feed_forward, between[0], ctx_rev, between[1], ssm_kernel, d_skip, padded)
        l0_feed_forward(core, to_feed_forward, to_causal, between[1], between[2], gate_s, up_s, down_s)
        core.clear()
        l1_attention(core, to_causal, to_cross, between[2], between[3], q_scale, k_scale)
        l1_cross(core, to_cross, to_experts, between[3], ctx, between[4], gamma)
        l1_experts(core, to_experts, between[4], out, wr, br, wdn, bd, wup, bu)


def kernel(x, ctx_2048, L0_attn_Wq, L0_attn_bq, L0_attn_Wk, L0_attn_bk, L0_attn_Wv, L0_attn_bv, L0_attn_Wo,
           L0_xattn_ssm_kernel, L0_xattn_D, L0_ffn_gate_w, L0_ffn_up_w, L0_ffn_down_w, L0_ffn_gate_s,
           L0_ffn_up_s, L0_ffn_down_s, L1_attn_Wqkv, L1_attn_q_ln_scale, L1_attn_k_ln_scale, L1_attn_out_W,
           L1_xattn_gamma, L1_ffn_Wr, L1_ffn_br, L1_ffn_Wd, L1_ffn_bd, L1_ffn_Wu, L1_ffn_bu):
    import numpy as np
    import concourse.bacc as bacc
    from concourse.bass_utils import run_bass_kernel_spmd as run

    def tokens(a):
        return np.asarray(a).reshape(B * S, D)

    def turned(a):
        return np.asarray(a).T

    def columns(a):
        return np.asarray(a).reshape(-1, P).T

    context = tokens(ctx_2048)
    laid_out = {
        "x": tokens(x), "ctx": context,
        "ctx_rev": context.reshape(B * S, D // P, P)[:, :, ::-1].reshape(B * S, D),
        "wqT": turned(L0_attn_Wq), "bq": columns(L0_attn_bq), "wkT": turned(L0_attn_Wk), "bk": L0_attn_bk,
        "wvT": turned(L0_attn_Wv), "bv": L0_attn_bv, "woT": turned(L0_attn_Wo),
        "ssm_kernel": L0_xattn_ssm_kernel, "d_skip": np.asarray(L0_xattn_D).reshape(HC, 1),
        "gateT": turned(L0_ffn_gate_w), "upT": turned(L0_ffn_up_w), "downT": turned(L0_ffn_down_w),
        "gate_s": columns(L0_ffn_gate_s), "up_s": columns(L0_ffn_up_s), "down_s": L0_ffn_down_s,
        "wqkv": L1_attn_Wqkv, "q_scale": L1_attn_q_ln_scale, "k_scale": L1_attn_k_ln_scale, "wout": L1_attn_out_W,
        "gamma": np.asarray(L1_xattn_gamma).reshape(1),
        "wr": L1_ffn_Wr, "br": L1_ffn_br,
        "wdn": np.asarray(L1_ffn_Wd).transpose(1, 0, 2).reshape(D, E * R), "bd": np.asarray(L1_ffn_bd).reshape(E * R),
        "wup": np.asarray(L1_ffn_Wu).reshape(E * R, D), "bu": L1_ffn_bu,
    }
    nc = bacc.Bacc("TRN2", target_bir_lowering=False, num_devices=1)
    arrays = {f"in_{name}": np.ascontiguousarray(a) for name, a in laid_out.items()}
    args = [nc.dram_tensor(name, a.shape, mybir.dt.from_np(a.dtype), kind="ExternalInput").ap()
            for name, a in arrays.items()]
    args.append(nc.dram_tensor("out_x", (B * S, D), F32, kind="ExternalOutput").ap())
    decoder(nc, *args)
    return run(nc, [arrays], core_ids=[0]).results[0]["out_x"].reshape(B, S, D)
```
